# Optimizing a Trainium2 kernel written in Bass

```python
import numpy as np
import jax
import jax.numpy as jnp

def _softmax(x, axis=-1):
    return jax.nn.softmax(x, axis=axis)

def _gelu(x):
    return jax.nn.gelu(x, approximate=True)

def _silu(x):
    return jax.nn.silu(x)

def _sigmoid(x):
    return jax.nn.sigmoid(x)

def _layernorm(x, axis=-1, eps=1e-05):
    m = jnp.mean(x, axis=axis, keepdims=True)
    v = jnp.var(x, axis=axis, keepdims=True)
    return (x - m) / jnp.sqrt(v + eps)

def _scatter_add(tgt, idx, src, axis=0):
    return tgt.at[idx].add(src)

def _segment_sum(src, seg, n):
    return jax.ops.segment_sum(src, seg, n)
kernel_name = 'mk_seq_preln_d1_jaxref_r8_598ebd'

def setup_inputs(seed: int=0):
    np.random.seed(seed)
    _w = jnp.asarray

    def _L0_attn_setup():
        import jax, jax.numpy as jnp
        import numpy as np
        D_MODEL = 128
        N_HEADS = 16
        HEAD_DIM = D_MODEL // N_HEADS
        WINDOW = 64
        PREFIX = 16
        B = 2
        S = 512

        def _windowed_global_attention(q, k, v):
            Bb, H, S_, Dh = q.shape
            W, P = (WINDOW, PREFIX)
            C = S_ // W
            scale = 1.0 / np.sqrt(Dh).astype(np.float32)
            qc = q.reshape(Bb, H, C, W, Dh)
            kp = jnp.pad(k, ((0, 0), (0, 0), (W, 0), (0, 0)))
            vp = jnp.pad(v, ((0, 0), (0, 0), (W, 0), (0, 0)))
            tail_idx = jnp.arange(C)[:, None] * W + jnp.arange(2 * W)[None, :]
            kt = kp[:, :, tail_idx, :]
            vt = vp[:, :, tail_idx, :]
            kg = k[:, :, :P, :]
            vg = v[:, :, :P, :]
            sg = jnp.einsum('bhcqd,bhkd->bhcqk', qc, kg) * scale
            st = jnp.einsum('bhcqd,bhckd->bhcqk', qc, kt) * scale
            q_pos = jnp.arange(C)[:, None] * W + jnp.arange(W)[None, :]
            kt_pos = jnp.arange(C)[:, None] * W - W + jnp.arange(2 * W)[None, :]
            mg = jnp.arange(P)[None, None, :] <= q_pos[:, :, None]
            diff = q_pos[:, :, None] - kt_pos[:, None, :]
            mt = (diff >= 0) & (diff < W) & (kt_pos[:, None, :] >= P)
            neg = jnp.asarray(-1000000000.0, sg.dtype)
            scores = jnp.concatenate([jnp.where(mg[None, None], sg, neg), jnp.where(mt[None, None], st, neg)], axis=-1)
            attn = jax.nn.softmax(scores, axis=-1)
            vcat = jnp.concatenate([jnp.broadcast_to(vg[:, :, None], (Bb, H, C, P, Dh)), vt], axis=3)
            out = jnp.einsum('bhcqk,bhckd->bhcqd', attn, vcat)
            return out.reshape(Bb, H, S_, Dh)
        key = jax.random.key(seed)
        k1, k2, k3 = jax.random.split(key, 3)
        x = jax.random.normal(k1, (B, S, D_MODEL), dtype=jnp.float32)
        w_qkv = jax.random.normal(k2, (3 * D_MODEL, D_MODEL), dtype=jnp.float32) * 0.02
        w_out = jax.random.normal(k3, (D_MODEL, D_MODEL), dtype=jnp.float32) * 0.02
        return {'x': x, 'w_qkv': w_qkv, 'w_out': w_out}
    _L0_attn_in = _L0_attn_setup()

    def _L0_ffn_setup():
        import jax, jax.numpy as jnp
        import numpy as np
        D = 128
        E = 8
        H = 256
        TOP_K = 2
        ALPHA = 0.5
        LN_EPS = 1e-05

        def _experts_all(x, W1, b1, W2, b2):
            h = jax.nn.relu(jnp.einsum('bld,edh->eblh', x, W1) + b1[:, None, None, :])
            return jnp.einsum('eblh,ehd->ebld', h, W2) + b2[:, None, None, :]

        def _selected_expert(x, expert_idx, W1, b1, W2, b2):
            oh = jax.nn.one_hot(expert_idx, E, dtype=x.dtype)
            return jnp.einsum('ebld,ble->bld', _experts_all(x, W1, b1, W2, b2), oh)

        def _layer_norm(x, gamma, beta):
            mu = jnp.mean(x, axis=-1, keepdims=True)
            var = jnp.mean(jnp.square(x - mu), axis=-1, keepdims=True)
            return (x - mu) * jax.lax.rsqrt(var + LN_EPS) * gamma + beta
        key = jax.random.key(seed)
        ks = jax.random.split(key, 8)
        x = jax.random.normal(ks[0], (2, 256, D), dtype=jnp.float32)
        gate_W = jax.random.normal(ks[1], (D, E), dtype=jnp.float32) * 0.02
        gate_b = jnp.zeros((E,), dtype=jnp.float32)
        W1 = jax.random.normal(ks[2], (E, D, H), dtype=jnp.float32) * 0.02
        b1 = jnp.zeros((E, H), dtype=jnp.float32)
        W2 = jax.random.normal(ks[3], (E, H, D), dtype=jnp.float32) * 0.02
        b2 = jnp.zeros((E, D), dtype=jnp.float32)
        ln_gamma = jnp.ones((D,), dtype=jnp.float32)
        ln_beta = jnp.zeros((D,), dtype=jnp.float32)
        return {'x': x, 'gate_W': gate_W, 'gate_b': gate_b, 'W1': W1, 'b1': b1, 'W2': W2, 'b2': b2, 'ln_gamma': ln_gamma, 'ln_beta': ln_beta}
    _L0_ffn_in = _L0_ffn_setup()
    _d = {'L0_attn_x': _L0_attn_in['x'], 'L0_attn_w_qkv': _L0_attn_in['w_qkv'], 'L0_attn_w_out': _L0_attn_in['w_out'], 'L0_ffn_gate_W': _L0_ffn_in['gate_W'], 'L0_ffn_gate_b': _L0_ffn_in['gate_b'], 'L0_ffn_W1': _L0_ffn_in['W1'], 'L0_ffn_b1': _L0_ffn_in['b1'], 'L0_ffn_W2': _L0_ffn_in['W2'], 'L0_ffn_b2': _L0_ffn_in['b2'], 'L0_ffn_ln_gamma': _L0_ffn_in['ln_gamma'], 'L0_ffn_ln_beta': _L0_ffn_in['ln_beta']}
    _x0 = _d['L0_attn_x']
    _d['L0_attn_x'] = jax.random.normal(jax.random.fold_in(jax.random.key(seed), 1), (2, 1024, 128), dtype=_x0.dtype)
    del _x0
    return _d

def reference(L0_attn_x, L0_attn_w_qkv, L0_attn_w_out, L0_ffn_gate_W, L0_ffn_gate_b, L0_ffn_W1, L0_ffn_b1, L0_ffn_W2, L0_ffn_b2, L0_ffn_ln_gamma, L0_ffn_ln_beta):

    def _L0_attn_ref(x, w_qkv, w_out):
        import jax, jax.numpy as jnp
        import numpy as np
        D_MODEL = 128
        N_HEADS = 16
        HEAD_DIM = D_MODEL // N_HEADS
        WINDOW = 64
        PREFIX = 16
        B = 2
        S = 512

        def _windowed_global_attention(q, k, v):
            Bb, H, S_, Dh = q.shape
            W, P = (WINDOW, PREFIX)
            C = S_ // W
            scale = 1.0 / np.sqrt(Dh).astype(np.float32)
            qc = q.reshape(Bb, H, C, W, Dh)
            kp = jnp.pad(k, ((0, 0), (0, 0), (W, 0), (0, 0)))
            vp = jnp.pad(v, ((0, 0), (0, 0), (W, 0), (0, 0)))
            tail_idx = jnp.arange(C)[:, None] * W + jnp.arange(2 * W)[None, :]
            kt = kp[:, :, tail_idx, :]
            vt = vp[:, :, tail_idx, :]
            kg = k[:, :, :P, :]
            vg = v[:, :, :P, :]
            sg = jnp.einsum('bhcqd,bhkd->bhcqk', qc, kg) * scale
            st = jnp.einsum('bhcqd,bhckd->bhcqk', qc, kt) * scale
            q_pos = jnp.arange(C)[:, None] * W + jnp.arange(W)[None, :]
            kt_pos = jnp.arange(C)[:, None] * W - W + jnp.arange(2 * W)[None, :]
            mg = jnp.arange(P)[None, None, :] <= q_pos[:, :, None]
            diff = q_pos[:, :, None] - kt_pos[:, None, :]
            mt = (diff >= 0) & (diff < W) & (kt_pos[:, None, :] >= P)
            neg = jnp.asarray(-1000000000.0, sg.dtype)
            scores = jnp.concatenate([jnp.where(mg[None, None], sg, neg), jnp.where(mt[None, None], st, neg)], axis=-1)
            attn = jax.nn.softmax(scores, axis=-1)
            vcat = jnp.concatenate([jnp.broadcast_to(vg[:, :, None], (Bb, H, C, P, Dh)), vt], axis=3)
            out = jnp.einsum('bhcqk,bhckd->bhcqd', attn, vcat)
            return out.reshape(Bb, H, S_, Dh)
        Bb, S_, Dm = x.shape
        qkv = x @ w_qkv.T
        q, k, v = jnp.split(qkv, 3, axis=-1)

        def heads(t):
            return t.reshape(Bb, S_, N_HEADS, HEAD_DIM).transpose(0, 2, 1, 3)
        q, k, v = (heads(q), heads(k), heads(v))
        o = _windowed_global_attention(q, k, v)
        o = o.transpose(0, 2, 1, 3).reshape(Bb, S_, Dm)
        return o @ w_out.T

    def _L0_ffn_ref(x, gate_W, gate_b, W1, b1, W2, b2, ln_gamma, ln_beta):
        import jax, jax.numpy as jnp
        import numpy as np
        D = 128
        E = 8
        H = 256
        TOP_K = 2
        ALPHA = 0.5
        LN_EPS = 1e-05

        def _experts_all(x, W1, b1, W2, b2):
            h = jax.nn.relu(jnp.einsum('bld,edh->eblh', x, W1) + b1[:, None, None, :])
            return jnp.einsum('eblh,ehd->ebld', h, W2) + b2[:, None, None, :]

        def _selected_expert(x, expert_idx, W1, b1, W2, b2):
            oh = jax.nn.one_hot(expert_idx, E, dtype=x.dtype)
            return jnp.einsum('ebld,ble->bld', _experts_all(x, W1, b1, W2, b2), oh)

        def _layer_norm(x, gamma, beta):
            mu = jnp.mean(x, axis=-1, keepdims=True)
            var = jnp.mean(jnp.square(x - mu), axis=-1, keepdims=True)
            return (x - mu) * jax.lax.rsqrt(var + LN_EPS) * gamma + beta
        residual = x
        gate_logits = jnp.einsum('bld,de->ble', x, gate_W) + gate_b
        gate_weights = jax.nn.softmax(gate_logits, axis=-1)
        topk_vals, topk_idx = jax.lax.top_k(gate_weights, TOP_K)
        boost = jax.lax.stop_gradient(x)
        outs = []
        for i in range(TOP_K):
            eo = _selected_expert(boost, topk_idx[:, :, i], W1, b1, W2, b2)
            outs.append(eo)
            if i < TOP_K - 1:
                boost = boost + ALPHA * jax.lax.stop_gradient(eo)
        fused = sum((topk_vals[:, :, i:i + 1] * outs[i] for i in range(TOP_K)))
        return _layer_norm(residual + fused, ln_gamma, ln_beta)
    x = L0_attn_x
    x = x + _L0_attn_ref(_layernorm(x, axis=-1), L0_attn_w_qkv, L0_attn_w_out)
    x = x + _L0_ffn_ref(_layernorm(x, axis=-1), L0_ffn_gate_W, L0_ffn_gate_b, L0_ffn_W1, L0_ffn_b1, L0_ffn_W2, L0_ffn_b2, L0_ffn_ln_gamma, L0_ffn_ln_beta)
    return x

_drawn_inputs = setup_inputs


def setup_inputs(seed=0):
    import zlib

    import numpy as np

    out = dict(_drawn_inputs(seed))
    spreads = {'L0_ffn_gate_b': (0.0, 0.8),
     'L0_ffn_b1': (0.0, 0.8),
     'L0_ffn_b2': (0.0, 0.706),
     'L0_ffn_ln_gamma': (1.0, 0.2),
     'L0_ffn_ln_beta': (0.0, 0.1)}
    factors = {'L0_attn_w_qkv': 8.0,
     'L0_attn_w_out': 8.0,
     'L0_ffn_gate_W': 4.955,
     'L0_ffn_W1': 8.0,
     'L0_ffn_W2': 8.0}
    for name, (base, spread) in spreads.items():
        noise = np.random.default_rng([zlib.crc32(name.encode()), seed]).standard_normal(out[name].shape)
        drawn = base * np.exp(spread * noise) if base else spread * noise
        out[name] = jnp.asarray(drawn.astype(out[name].dtype))
    for name, factor in factors.items():
        out[name] = (out[name] * factor).astype(out[name].dtype)
    return out
```

```python
import concourse.bass as bass
from concourse import mybir
from contextlib import ExitStack


def preln_block_kernel(nc, x, wqkvT, woT, gateW, gateb, W1, b1T, W2, b2, gamma, beta,
                       ident, identb, kconst, qconst, maxsel, prefmask, prefmaskT,
                       headsel, selgrp, b1sel, ohsel, partsel, out):
    fp32 = mybir.dt.float32
    bf16 = mybir.dt.bfloat16
    ALU = mybir.AluOpType
    ACT = mybir.ActivationFunctionType
    AX = mybir.AxisListType

    D = 128
    NH, HD = 16, 8
    SEQ = 1024
    W, PRE = 64, 16
    ST = 512
    NS = 4
    NT = ST // 128
    NC = ST // W
    E, HID = 8, 256
    NB = E * (HID // 128)
    NPROD = 6
    ROWS = NPROD * HD
    MROW = ROWS + 1
    EPS = 1e-5
    SCALE = float(HD) ** -0.5
    QPARTS = [0, 0, 1, 0, 2, 1]
    KPARTS = [0, 1, 0, 2, 0, 1]
    XM = 64

    qd = nc.dram_tensor("qstack", [NS, NPROD, HD, NH, ST], bf16).ap()
    kd = nc.dram_tensor("kstack", [NS // 2, NPROD, HD, NH, SEQ], bf16).ap()

    ctx = ExitStack()
    with ctx:
        def sb(name, shape, dt=fp32):
            return ctx.enter_context(nc.sbuf_tensor(name, shape, dt))

        def sem(name):
            return ctx.enter_context(nc.semaphore(name))

        wqkv_s = sb("wqkv_s", [128, 3 * D])
        wo_s = sb("wo_s", [128, D])
        gw_s = sb("gw_s", [128, E])
        gb_s = sb("gb_s", [128, E])
        w1_s = sb("w1_s", [128, E, HID])
        w2_s = sb("w2_s", [128, NB, D])
        b1_s = sb("b1_s", [128, NB])
        nb1_s = sb("nb1_s", [128, NB])
        b2_s = sb("b2_s", [24, D])
        gam_s = sb("gam_s", [128, D])
        bet_s = sb("bet_s", [128, D])
        id_s = sb("id_s", [128, 128])
        idb_s = sb("idb_s", [128, 128], bf16)
        msel_s = sb("msel_s", [NH, 2, 128], bf16)
        pm_s = sb("pm_s", [128, NH * PRE], bf16)
        pmT_s = sb("pmT_s", [128, 128], bf16)
        hsel_s = sb("hsel_s", [128, NH])
        gsel_s = sb("gsel_s", [128, NH])
        ohsel_s = sb("ohsel_s", [24, E, 128], bf16)
        psel_s = sb("psel_s", [24, 3])
        epsm_s = sb("epsm_s", [128, NT])
        iota_s = sb("iota_s", [128, E])
        c24 = sb("c24", [24, D])
        c24h = sb("c24h", [24, D], bf16)
        c24r = sb("c24r", [24, D])
        c24m = sb("c24m", [24, D], bf16)
        c24l = sb("c24l", [24, D])
        c24t = sb("c24t", [24, D])
        cpart = sb("cpart", [24, D], bf16)
        x_s = sb("x_s", [128, NS, NT, D])
        st6 = sb("st6", [128, NT, 6])
        mv = sb("mv", [128, NT, 2])
        veps = sb("veps", [128, NT])
        rstd = sb("rstd", [128, NT])
        xn = sb("xn", [128, NT, D])
        xnT = sb("xnT", [128, 2, XM + ST])
        kf = sb("kf", [128, ST])
        qf = sb("qf", [128, 2, ST])
        kp = sb("kp", [128, 3, ST], bf16)
        qp = sb("qp", [128, 3, ST], bf16)
        kr = sb("kr", [128, ST])
        qr = sb("qr", [128, ST])
        xg = sb("xg", [128, 8, PRE])
        kg = sb("kg", [128, 2, NH, PRE])
        vg = sb("vg", [128, 2, 4, 4, 32])
        vaug = sb("vaug", [128, 2, 2, NT, NH, HD + 1])
        QS = sb("QS", [128, 2, NH, ST], bf16)
        KS = sb("KS", [128, 2, NH, NC, 2 * W], bf16)
        m4 = sb("m4", [128, NT, NH])
        mg = sb("mg", [128, NT, NH])
        mt = sb("mt", [128, NT, NH])
        mh = sb("mh", [NH, ST], bf16)
        ml = sb("ml", [NH, ST], bf16)
        PG = sb("PG", [128, 2, ST])
        PT = sb("PT", [128, 2, NH, W])
        early = PT[:, :].rearrange("p a h q -> p (a h q)").bitcast(bf16)
        kc_s = early[:, 0:4 * ST].rearrange("p (a t) -> p a t", a=2)
        qc_s = early[:, 4 * ST:5 * ST]
        oS = sb("oS", [128, 2, 4, 256])
        rden = sb("rden", [128, 2, NH])
        otok = sb("otok", [128, 2, NH, HD])
        oT = sb("oT", [128, 2, D])
        xn2 = sb("xn2", [128, NT, D])
        xn2T = sb("xn2T", [128, ST])
        lg = sb("lg", [128, NT, E])
        lg2 = sb("lg2", [128, NT, E])
        tmp8 = sb("tmp8", [128, NT, E])
        pk = sb("pk", [128, NT, 2])
        top = sb("top", [128, NT, 2])
        oh = sb("oh", [128, 2, NT, 3, E])
        dif = sb("dif", [128, NT, E + 1])
        ex = sb("ex", [128, NT, E + 1])
        dn = sb("dn", [128, NT])
        rdn = sb("rdn", [128, NT])
        val = sb("val", [128, NT, 2])
        ohT = sb("ohT", [24, 2, ST], bf16)
        ohB = sb("ohB", [128, 4, ST], bf16)
        boost = kr
        yS = PG
        b1d_s = PG[:, 0, 0:NB * 24].rearrange("p (i c) -> p i c", i=NB)
        hid = oS[:, :, :, :].rearrange("p a g q -> p (a g q)").rearrange("p (i t) -> p i t", i=4)
        z = sb("z", [128, NT, D])
        b1sel_s = z[:, :, :].rearrange("p t d -> p (t d)")[:, 0:NB * 24].rearrange("p (i c) -> p i c", i=NB)

        pb = [ctx.enter_context(nc.psum_tensor(f"bank{i}", [128, 512], fp32)) for i in range(2)]
        ring = ctx.enter_context(nc.psum_tensor("ring", [128, 4, 512], fp32))
        pa = [ctx.enter_context(nc.psum_tensor(f"aux{i}", [128, 512], fp32)) for i in range(2)]

        names = """w_in x_in0 x_in1 x_in2 x_in3 c_in i_in f_in st_init vones stats rstd_ok xn_ok xnT_ps xnT_ok k_ps q_ps v_ps
            vg_ps kf_ok qf_ok v_ok vg_ok kg_ok xg_ok kparts qparts kd_wr qd_wr ks_in qs_in s1_ps g1_ps max_ok
            gmax_ok mt_ok mT_ps mhl m_in pg_ps pg_ok s2_ps pt_ok pv_ok oS_ok oT_ps otok_ok o2_ps oT_ok
            att_ps x1_ok stats2 rstd2_ok xn2_ok xn2T_ps xn2T_ok lg_ps oh_ok ohT_ps ohT_ok ohB_ps ohB_ok
            c_ps c_ok b1d_ok h_ps h_ok h_used dif_ok ex_ok boost_ok yS_ok yT_ps z_ok stats3 rstd3_ok outs_ok out_wr
            dchain pchain""".split()
        s = {n: sem(n) for n in names}
        block = ctx.enter_context(nc.Block())

        def stage_order(A, C, Dd, Ee, F):
            A(0)
            C(0)
            for n in range(NS):
                if n + 1 < NS:
                    A(n + 1)
                Dd(n)
                Ee(n)
                if n + 1 < NS:
                    C(n + 1)
                F(n)

        def nothing(n):
            pass

        xv = x.rearrange("(s t p) d -> s p t d", t=NT, p=128)
        ov = out.rearrange("(s t p) d -> s p t d", t=NT, p=128)

        @block.sync
        def _(sp):
            sp.dma_start(id_s[:, :], ident).then_inc(s["i_in"], 16)
            for n in range(NS):
                sp.dma_start(x_s[:, n], xv[n]).then_inc(s[f"x_in{n}"], 16)
                if n == 0:
                    sp.dma_start(wqkv_s[:, :], wqkvT).then_inc(s["w_in"], 16)
                    sp.dma_start(wo_s[:, :], woT).then_inc(s["w_in"], 16)
                    sp.dma_start(hsel_s[:, :], headsel).then_inc(s["w_in"], 16)
                    sp.dma_start(gsel_s[:, :], selgrp).then_inc(s["w_in"], 16)
            sp.wait_ge(s["st_init"], 2)

            def stacks(n):
                slot, b, c0 = n % 2, n // 2, (n % 2) * ST
                sp.wait_ge(s["kparts"], n + 1)
                for j, p in enumerate(KPARTS):
                    sp.dma_start(kd[b, j, :, :, c0:c0 + ST].rearrange("d h t -> h d t"),
                                 kp[:, p, :]).then_inc(s["kd_wr"], 16)
                sp.wait_ge(s["qparts"], n + 1)
                for j, p in enumerate(QPARTS):
                    sp.dma_start(qd[n, j].rearrange("d h t -> h d t"), qp[:, p, :]).then_inc(s["qd_wr"], 16)
                if n >= 2:
                    sp.wait_ge(s["s2_ps"], NC * (n - 1))
                sp.wait_ge(s["kd_wr"], 96 * (n + 1))
                kv = kd[b].rearrange("j d h t -> (j d) h t")
                for c in range(NC):
                    if c0 + c == 0:
                        src, dst = kv[:, :, 0:W], KS[0:ROWS, slot, :, c, W:2 * W]
                    else:
                        src, dst = kv[:, :, c0 + (c - 1) * W:c0 + (c + 1) * W], KS[0:ROWS, slot, :, c, :]
                    sp.dma_start(dst, src).then_inc(s["ks_in"], 16)
                sp.wait_ge(s["qd_wr"], 96 * (n + 1))
                sp.dma_start(QS[0:ROWS, slot, :, :], qd[n].rearrange("j d h t -> (j d) h t"))\
                    .then_inc(s["qs_in"], 16)
                sp.dma_start(QS[MROW:MROW + 2, slot, :, :],
                             qconst[MROW:MROW + 2, None, :].broadcast_to((2, NH, ST))).then_inc(s["qs_in"], 16)

            def maxima(n):
                sp.wait_ge(s["mhl"], 2 * (n + 1))
                sp.dma_start(QS[MROW:MROW + 1, n % 2, :, :], mh[:, :]).then_inc(s["m_in"], 16)
                sp.dma_start(QS[MROW + 1:MROW + 2, n % 2, :, :], ml[:, :]).then_inc(s["m_in"], 16)

            def store(n):
                sp.wait_ge(s["outs_ok"], n + 1)
                sp.dma_start(ov[n], z[:, :, :]).then_inc(s["out_wr"], 16)

            stage_order(stacks, maxima, nothing, nothing, store)
            sp.wait_ge(s["out_wr"], 16 * NS)

        @block.gpsimd
        def _(pool):
            count = [0]

            def link(ins):
                count[0] += 1
                ins.then_inc(s["pchain"], 1)
                pool.wait_ge(s["pchain"], count[0])

            nc.gpsimd.memset(xnT[:, 0, 0:XM], 0.0).then_inc(s["vones"], 1)
            nc.gpsimd.memset(vg[:], 0.0).then_inc(s["vones"], 1)
            nc.gpsimd.memset(vaug[:], 1.0).then_inc(s["vones"], 1)
            link(nc.gpsimd.memset(epsm_s[:, :], -0.5))

            def inv_std(var_ok, n, done):
                pool.wait_ge(s[var_ok], n + 1)
                link(nc.gpsimd.tensor_scalar(veps[:, :], mv[:, :, 1], EPS, None, ALU.add))
                nc.gpsimd.tensor_tensor(rstd[:, :], veps[:, :], epsm_s[:, :], ALU.pow).then_inc(s[done], 1)

            def A(n):
                inv_std("stats", n, "rstd_ok")
                pool.wait_ge(s["qf_ok"], n + 1)
                if n >= 1:
                    pool.wait_ge(s["qd_wr"], 96 * n)
                q = qf[:, n % 2, :]
                link(nc.gpsimd.tensor_copy(qp[:, 0, :], q))
                link(nc.gpsimd.tensor_tensor(qr[:, :], q, qp[:, 0, :], ALU.subtract))
                link(nc.gpsimd.tensor_copy(qp[:, 1, :], qr[:, :]))
                nc.gpsimd.tensor_tensor(qp[:, 2, :], qr[:, :], qp[:, 1, :], ALU.subtract)\
                    .then_inc(s["qparts"], 1)

            def Ee(n):
                inv_std("stats2", n, "rstd2_ok")

            def F(n):
                inv_std("stats3", n, "rstd3_ok")

            stage_order(A, nothing, nothing, Ee, F)

        @block.scalar
        def _(act):
            cs = [(kc_s[:, :, :], kconst), (qc_s[:, :], qconst), (idb_s[:, :], identb),
                  (pm_s[:, :], prefmask), (pmT_s[:, :], prefmaskT), (msel_s[:, :, :], maxsel)]
            for dst, src in cs:
                act.dma_start(dst, src).then_inc(s["c_in"], 16)
            fs = [(gw_s[:, :], gateW), (gb_s[:, :], gateb[None, :].broadcast_to((128, E))),
                  (gam_s[:, :], gamma[None, :].broadcast_to((128, D))),
                  (bet_s[:, :], beta[None, :].broadcast_to((128, D))),
                  (w1_s[:, :, :], W1.rearrange("e d h -> d e h")),
                  (w2_s[:, :, :], W2.rearrange("e (b p) d -> p (e b) d", p=128)),
                  (b1_s[:, :], b1T), (b1sel_s[:, :, :], b1sel), (ohsel_s[:, :, :], ohsel), (psel_s[:, :], partsel)]
            for dst, src in fs:
                act.dma_start(dst, src).then_inc(s["f_in"], 16)
            for i in range(3):
                act.dma_start(b2_s[8 * i:8 * i + 8, :], b2).then_inc(s["f_in"], 16)

            def A(n):
                slot = n % 2
                act.wait_ge(s["xnT_ps"], n + 1)
                if n == 0:
                    act.wait_ge(s["vones"], 3)
                if n >= 2:
                    act.wait_ge(s["v_ps"], 2 * (n - 1))
                if slot == 0:
                    if n >= 2:
                        act.wait_ge(s["v_ps"], 2 * n)
                        act.wait_ge(s["xg_ok"], n // 2)
                    nc.scalar.copy(xnT[:, 1, 0:XM], pa[0][:, ST - XM:ST]).then_inc(s["xnT_ok"], 1)
                nc.scalar.copy(xnT[:, slot, XM:XM + ST], pa[0][:, :]).then_inc(s["xnT_ok"], 1)
                act.wait_ge(s["k_ps"], n + 1)
                if n >= 1:
                    act.wait_ge(s["kparts"], n)
                nc.scalar.copy(kf[:, :], pa[1][:, :]).then_inc(s["kf_ok"], 1)
                act.wait_ge(s["q_ps"], n + 1)
                if n >= 2:
                    act.wait_ge(s["pg_ps"], 2 * (n - 1))
                    act.wait_ge(s["qparts"], n - 1)
                nc.scalar.mul(qf[:, slot, :], pa[0][:, :], SCALE).then_inc(s["qf_ok"], 1)
                if n >= 2:
                    act.wait_ge(s["pv_ok"], NC * (n - 1))
                for k in range(2):
                    act.wait_ge(s["v_ps"], 2 * n + k + 1)
                    nc.scalar.copy(vaug[:, slot, k, :, :, 0:HD],
                                   pa[1 - k][:, :].rearrange("p (t h d) -> p t h d", t=NT, d=HD))\
                        .then_inc(s["v_ok"], 1)

            def Dd(n):
                slot = n % 2
                for g in range(2):
                    act.wait_ge(s["pg_ps"], 2 * n + g + 1)
                    if n >= 1:
                        act.wait_ge(s["yT_ps"], 2 * n)
                    nc.scalar.activation(PG[:, g, :], pa[g][:, :], ACT.Exp).then_inc(s["pg_ok"], 1)
                for c in range(NC):
                    i = NC * n + c
                    act.wait_ge(s["s2_ps"], i + 1)
                    if i >= 2:
                        act.wait_ge(s["pv_ok"], i - 1)
                    nc.scalar.activation(PT[:, i % 2].rearrange("p (g h) q -> p g (h q)", g=2),
                                         ring[:, 2 * (i % 2):2 * (i % 2) + 2, :], ACT.Exp)\
                        .then_inc(s["pt_ok"], 1)

            def Ee(n):
                for t in range(NT):
                    i = NT * n + t
                    act.wait_ge(s["o2_ps"], i + 1)
                    if i >= 2:
                        act.wait_ge(s["att_ps"], i - 1)
                    nc.scalar.copy(oT[:, i % 2, :], ring[:, t, 0:D]).then_inc(s["oT_ok"], 1)
                act.wait_ge(s["xn2T_ps"], n + 1)
                if n >= 1:
                    act.wait_ge(s["h_ps"], 2 * NB * n)
                    act.wait_ge(s["boost_ok"], n)
                nc.scalar.copy(xn2T[:, :], pa[0][:, :]).then_inc(s["xn2T_ok"], 1)

            def F(n):
                act.wait_ge(s["dif_ok"], n + 1)
                nc.scalar.activation(ex[:, :, :], dif[:, :, :], ACT.Exp).then_inc(s["ex_ok"], 1)
                for r in range(2):
                    for e in range(E):
                        i = (2 * n + r) * E + e
                        act.wait_ge(s["ohB_ps"], i + 1)
                        if i >= 4:
                            act.wait_ge(s["h_ok"], 2 * (i - 3))
                        nc.scalar.copy(ohB[:, i % 4, :], pa[e % 2][:, :]).then_inc(s["ohB_ok"], 1)
                for r in range(2):
                    act.wait_ge(s["h_used"], NB * (2 * n + r + 1))
                    if n >= 1:
                        act.wait_ge(s["yT_ps"], 2 * n)
                    if r == 0:
                        act.wait_ge(s["boost_ok"], n + 1)
                    nc.scalar.copy(yS[:, r, :], pb[r][:, :]).then_inc(s["yS_ok"], 1)

            stage_order(A, nothing, Dd, Ee, F)

        @block.tensor
        def _(pe):
            mm = nc.tensor.matmul

            def A(n):
                slot = n % 2
                if n == 0:
                    pe.wait_ge(s["i_in"], 16)
                else:
                    if n >= 2:
                        pe.wait_ge(s["z_ok"], 2 * (n - 1))
                    pe.wait_ge(s["mhl"], 2 * n)
                    pe.wait_ge(s["gmax_ok"], NT * n)
                pe.wait_ge(s["xn_ok"], NT * (n + 1))
                for t in range(NT):
                    last = nc.tensor.transpose(pa[0][:, t * 128:(t + 1) * 128], xn[:, t, :], id_s[:, :])
                last.then_inc(s["xnT_ps"], 1)
                pe.wait_ge(s["xnT_ok"], n + 1 + n // 2 + 1)
                if n == 0:
                    pe.wait_ge(s["w_in"], 64)
                xt = xnT[:, slot, XM:XM + ST]
                mm(pa[1][:, :], wqkv_s[:, D:2 * D], xt, start=True, stop=True).then_inc(s["k_ps"], 1)
                mm(pa[0][:, :], wqkv_s[:, 0:D], xt, start=True, stop=True).then_inc(s["q_ps"], 1)
                for k in range(2):
                    pe.wait_ge(s["kf_ok" if k == 0 else "qf_ok"], n + 1)
                    for t in range(NT):
                        c = t * 128 + (XM if k == 0 else 0)
                        last = mm(pa[1 - k][:, t * 128:(t + 1) * 128], xnT[:, slot, c:c + 128],
                                  wqkv_s[:, 2 * D:3 * D], start=True, stop=True)
                    last.then_inc(s["v_ps"], 1)
                if slot == 0:
                    pe.wait_ge(s["xg_ok"], n // 2 + 1)
                    pe.wait_ge(s["v_ok"], 2 * n + 1)
                    mm(pa[1][:, 0:D], xg[:, :, :].rearrange("p a k -> p (a k)"), wqkv_s[:, 2 * D:3 * D],
                       start=True, stop=True).then_inc(s["vg_ps"], 1)

            def window(slot, h, c):
                return KS[:, slot, h, c, :]

            def C(n):
                slot, b = n % 2, n // 2
                if n == 0:
                    pe.wait_ge(s["c_in"], 96)
                    pe.wait_ge(s["st_init"], 2)
                pe.wait_ge(s["ks_in"], 16 * NC * (n + 1))
                pe.wait_ge(s["qs_in"], 32 * (n + 1))
                pe.wait_ge(s["kg_ok"], b + 1)
                pe.wait_ge(s["v_ok"], 2 * (n + 1))
                pe.wait_ge(s["vg_ok"], 2 * (b + 1))
                if n >= 1:
                    pe.wait_ge(s["x1_ok"], NT * n)
                    pe.wait_ge(s["xn2T_ok"], n)
                for t in range(NT):
                    for g in range(4):
                        i = (NT * n + t) * 4 + g
                        if t >= 1:
                            pe.wait_ge(s["max_ok"], i - 3)
                        for hh in range(4):
                            for p in range(2):
                                c = 2 * t + p
                                h = 4 * g + hh
                                last = mm(ring[W * p:W * (p + 1), g, hh * 128:(hh + 1) * 128],
                                          QS[:, slot, h, c * W:(c + 1) * W], window(slot, h, c),
                                          start=(hh == 0), stop=True, skip_group_check=True)
                        last.then_inc(s["s1_ps"], 1)
                    if t >= 2:
                        pe.wait_ge(s["gmax_ok"], NT * n + t - 1)
                    first = slot == 0 and t == 0
                    last = mm(pa[t % 2][:, 0:NH * PRE], qf[:, slot, t * 128:(t + 1) * 128],
                              kg[:, b].rearrange("p h k -> p (h k)"), start=True, stop=not first)
                    if first:
                        last = mm(pa[t % 2][:, 0:NH * PRE], idb_s[:, :], pm_s[:, :], start=False, stop=True)
                    last.then_inc(s["g1_ps"], 1)
                pe.wait_ge(s["mt_ok"], n + 1)
                for t in range(NT):
                    last = nc.tensor.transpose(pa[0][0:NH, t * 128:(t + 1) * 128], mt[:, t, :], id_s[:, :])
                last.then_inc(s["mT_ps"], 1)

            def Dd(n):
                slot, b = n % 2, n // 2
                if n >= 1:
                    pe.wait_ge(s["yS_ok"], 2 * n)
                    pe.wait_ge(s["z_ok"], 2 * n)
                    pe.wait_ge(s["h_ok"], 2 * NB * n)
                if n + 1 < NS:
                    pe.wait_ge(s["v_ok"], 2 * (n + 2))
                    pe.wait_ge(s["vg_ok"], 2 * ((n + 1) // 2 + 1))
                pe.wait_ge(s["mhl"], 2 * (n + 1))
                pe.wait_ge(s["max_ok"], 4 * NT * (n + 1))
                for g in range(2):
                    dst = pa[g]
                    mm(dst[:, :], kg[:, b, 8 * g:8 * g + 8].rearrange("p h k -> p (h k)"), qf[:, slot, :],
                       start=True, stop=False)
                    mm(dst[:, :], msel_s[:, g, :], mh[:, :], start=False, stop=False)
                    if slot == 0:
                        mm(dst[:, 0:PRE], pmT_s[:, :], idb_s[:, 0:PRE], start=False, stop=False)
                    mm(dst[:, :], msel_s[:, g, :], ml[:, :], start=False, stop=True).then_inc(s["pg_ps"], 1)
                pe.wait_ge(s["m_in"], 32 * (n + 1))

                def scores(c):
                    i = NC * n + c
                    if i >= 2:
                        pe.wait_ge(s["pt_ok"], i - 1)
                    for h in range(NH):
                        last = mm(ring[:, 2 * (i % 2) + h // 8, (h % 8) * W:(h % 8 + 1) * W],
                                  window(slot, h, c), QS[:, slot, h, c * W:(c + 1) * W],
                                  start=(h % 8 == 0), stop=True, skip_group_check=True)
                    last.then_inc(s["s2_ps"], 1)

                def values(c):
                    i = NC * n + c
                    pe.wait_ge(s["pt_ok"], i + 1)
                    if c % 4 == 0:
                        if i >= 4:
                            pe.wait_ge(s["oS_ok"], i // 4)
                        for g in range(4):
                            mm(pb[g // 2][:, (g % 2) * 256:(g % 2 + 1) * 256],
                               vg[:, b, g].rearrange("p i e -> p (i e)"),
                               PG[:, g // 2, (c // 4) * 256:(c // 4 + 1) * 256],
                               start=(g % 2 == 0), stop=True, skip_group_check=True)
                    for h in range(NH):
                        g, q = h // 4, h % 4
                        col = (g % 2) * 256 + (c % 4) * W
                        last = mm(pb[g // 2][32 * q:32 * q + HD + 1, col:col + W],
                                  vaug[:, slot, 0 if c % 2 else 1, c // 2, h, :], PT[:, i % 2, h, :],
                                  start=False, stop=True, skip_group_check=True)
                    last.then_inc(s["pv_ok"], 1)

                scores(0)
                pe.wait_ge(s["pg_ok"], 2 * (n + 1))
                for c in range(NC):
                    if c + 1 < NC:
                        scores(c + 1)
                    values(c)

            def Ee(n):
                pe.wait_ge(s["pt_ok"], NC * (n + 1))
                for t in range(NT):
                    i = NT * n + t
                    if t % 2 == 0:
                        pe.wait_ge(s["oS_ok"], 2 * n + t // 2 + 1)
                    if t >= 2:
                        pe.wait_ge(s["otok_ok"], i - 1)
                    for g in range(4):
                        last = nc.tensor.transpose(pa[t % 2][:, g * 128:(g + 1) * 128],
                                                   oS[:, t // 2, g, (t % 2) * 128:(t % 2 + 1) * 128], id_s[:, :])
                    last.then_inc(s["oT_ps"], 1)
                    if t >= 1:
                        back(i - 1)
                    if t >= 2:
                        project(i - 2)
                back(NT * n + 3)
                project(NT * n + 2)
                project(NT * n + 3)
                pe.wait_ge(s["xn2_ok"], NT * (n + 1))
                for t in range(NT):
                    last = nc.tensor.transpose(pa[0][:, t * 128:(t + 1) * 128], xn2[:, t, :], id_s[:, :])
                last.then_inc(s["xn2T_ps"], 1)

            def back(i):
                pe.wait_ge(s["otok_ok"], i + 1)
                nc.tensor.transpose(ring[:, i % 4, 0:D], otok[:, i % 2].rearrange("p h d -> p (h d)"), id_s[:, :])\
                    .then_inc(s["o2_ps"], 1)

            def project(i):
                pe.wait_ge(s["oT_ok"], i + 1)
                mm(ring[:, i % 4, D:2 * D], oT[:, i % 2, :], wo_s[:, :], start=True, stop=True)\
                    .then_inc(s["att_ps"], 1)

            def F(n):
                if n == 0:
                    pe.wait_ge(s["f_in"], 13 * 16)
                    pe.wait_ge(s["b1d_ok"], 1)
                    pe.wait_ge(s["oS_ok"], 2)
                    for i in range(NB):
                        last = mm(pb[0][0:24, 0:D], b1d_s[:, i, :], w2_s[:, i, :], start=(i == 0), stop=(i == NB - 1))
                    last.then_inc(s["c_ps"], 1)
                pe.wait_ge(s["xn2T_ok"], n + 1)
                if n + 1 < NS:
                    pe.wait_ge(s["mhl"], 2 * (n + 2))
                    pe.wait_ge(s["gmax_ok"], NT * (n + 2))
                    pe.wait_ge(s["max_ok"], 4 * NT * (n + 2))
                pe.wait_ge(s["otok_ok"], NT * (n + 1))
                for t in range(NT):
                    last = mm(pa[1][:, t * E:(t + 1) * E], xn2T[:, t * 128:(t + 1) * 128], gw_s[:, :],
                              start=True, stop=True)
                last.then_inc(s["lg_ps"], 1)
                for r in range(2):
                    pe.wait_ge(s["oh_ok"], n + 1)
                    for t in range(NT):
                        last = nc.tensor.transpose(pa[r][0:24, t * 128:(t + 1) * 128],
                                                   oh[:, r, t].rearrange("p j e -> p (j e)"), id_s[:, :])
                    last.then_inc(s["ohT_ps"], 1)
                pe.wait_ge(s["ohT_ok"], 2 * (n + 1))

                def spread(r, e):
                    i = (2 * n + r) * E + e
                    if r or e >= 2:
                        pe.wait_ge(s["ohB_ok"], i - 1)
                    mm(pa[e % 2][:, :], ohsel_s[:, e, :], ohT[:, r, :], start=True, stop=True)\
                        .then_inc(s["ohB_ps"], 1)

                spread(0, 0)
                spread(0, 1)
                if n == 0:
                    pe.wait_ge(s["c_ok"], 1)
                pe.wait_ge(s["oS_ok"], 2 * (n + 1))
                for r in range(2):
                    mm(pb[r][:, :], cpart[:, :], ohT[:, r, :], start=True, stop=False)
                    src = xn2T if r == 0 else boost
                    if r == 1:
                        pe.wait_ge(s["boost_ok"], n + 1)

                    def down(j):
                        i = (2 * n + r) * NB + j
                        pe.wait_ge(s["h_ok"], i + 1)
                        last = mm(pb[r][:, :], w2_s[:, j, :], hid[:, i % 4, :], start=False, stop=(j == NB - 1))
                        last.then_inc(s["h_used"], 1)

                    for j in range(NB):
                        i = (2 * n + r) * NB + j
                        if j >= 4 or r == 1:
                            pe.wait_ge(s["h_ok"], i - 3)
                        mm(ring[:, i % 4, :], w1_s[:, j // 2, (j % 2) * 128:(j % 2 + 1) * 128], src[:, :],
                           start=True, stop=True).then_inc(s["h_ps"], 1)
                        if j >= 2:
                            down(j - 2)
                        if j % 2 == 1:
                            nxt = (r * E + j // 2 + 2)
                            if nxt < 2 * E:
                                spread(nxt // E, nxt % E)
                    down(NB - 2)
                    down(NB - 1)
                for r in range(2):
                    pe.wait_ge(s["yS_ok"], 2 * n + r + 1)
                    pe.wait_ge(s["ohB_ok"], 2 * E * (n + 1))
                    for t in range(NT):
                        last = nc.tensor.transpose(pa[r][:, t * 128:(t + 1) * 128],
                                                   yS[:, r, t * 128:(t + 1) * 128], id_s[:, :])
                    last.then_inc(s["yT_ps"], 1)

            stage_order(A, C, Dd, Ee, F)

        @block.vector
        def _(dve):
            v = nc.vector
            count = [0]

            def link(ins):
                count[0] += 1
                ins.then_inc(s["dchain"], 1)
                dve.wait_ge(s["dchain"], count[0])

            def stats(src, n, var_ok):
                for t in range(NT):
                    link(v.bn_stats(st6[:, t, :], src(t)))
                for t in range(NT):
                    last = v.bn_aggr(mv[:, t, :], st6[:, t, :])
                last.then_inc(s[var_ok], 1)

            def A(n):
                if n == 1:
                    dve.wait_ge(s["mhl"], 2)
                if n >= 1:
                    dve.wait_ge(s["xnT_ps"], n)
                if n >= 2:
                    dve.wait_ge(s["outs_ok"], n - 1)
                dve.wait_ge(s[f"x_in{n}"], 16)
                stats(lambda t: x_s[:, n, t, :], n, "stats")
                dve.wait_ge(s["rstd_ok"], n + 1)
                dve.wait_ge(s["stats"], n + 1)
                for t in range(NT):
                    v.tensor_scalar(xn[:, t, :], x_s[:, n, t, :], mv[:, t, 0:1], rstd[:, t:t + 1],
                                    ALU.subtract, ALU.mult).then_inc(s["xn_ok"], 1)
                if n == 0:
                    dve.wait_ge(s["c_in"], 96)
                    for slot in range(2):
                        v.tensor_copy(KS[:, slot].rearrange("p h c k -> p h (c k)"),
                                      kc_s[:, None, slot, :].broadcast_to((128, NH, 2 * ST)))
                        last = v.tensor_copy(QS[:, slot, :, :], qc_s[:, None, :].broadcast_to((128, NH, ST)))
                        last.then_inc(s["st_init"], 1)
                if n % 2 == 0:
                    dve.wait_ge(s["xnT_ok"], n + 1 + n // 2 + 1)
                    if n >= 2:
                        dve.wait_ge(s["vg_ps"], n // 2)
                    v.tensor_copy(xg[:, :, :], xnT[:, 0, None, XM:XM + PRE].broadcast_to((128, 8, PRE)))\
                        .then_inc(s["xg_ok"], 1)
                dve.wait_ge(s["kf_ok"], n + 1)
                if n % 2 == 0:
                    if n == 0:
                        dve.wait_ge(s["w_in"], 64)
                    v.tensor_tensor(kg[:, n // 2], kf[:, None, 0:PRE].broadcast_to((128, NH, PRE)),
                                    hsel_s[:, :, None].broadcast_to((128, NH, PRE)), ALU.mult)\
                        .then_inc(s["kg_ok"], 1)
                if n >= 1:
                    dve.wait_ge(s["kd_wr"], 96 * n)
                link(v.tensor_copy(kp[:, 0, :], kf[:, :]))
                link(v.tensor_tensor(kr[:, :], kf[:, :], kp[:, 0, :], ALU.subtract))
                link(v.tensor_copy(kp[:, 1, :], kr[:, :]))
                v.tensor_tensor(kp[:, 2, :], kr[:, :], kp[:, 1, :], ALU.subtract).then_inc(s["kparts"], 1)
                if n % 2 == 0:
                    b = n // 2
                    dve.wait_ge(s["vg_ps"], b + 1)
                    dve.wait_ge(s["vones"], 3)
                    v.tensor_tensor(vg[:, b, :, :, 0:HD].rearrange("p g i d -> p (g i) d"),
                                    pa[1][:, 0:D].rearrange("p (h d) -> p h d", d=HD),
                                    gsel_s[:, :, None].broadcast_to((128, NH, HD)), ALU.mult)\
                        .then_inc(s["vg_ok"], 1)
                    v.tensor_copy(vg[:, b, :, :, HD].rearrange("p g i -> p (g i)"), gsel_s[:, :])\
                        .then_inc(s["vg_ok"], 1)

            def C(n):
                if n >= 1:
                    dve.wait_ge(s["mt_ok"], n)
                    dve.wait_ge(s["xn2_ok"], NT * n)
                for t in range(NT):
                    for g in range(4):
                        i = (NT * n + t) * 4 + g
                        dve.wait_ge(s["s1_ps"], i + 1)
                        v.tensor_reduce(m4[:, t, 4 * g:4 * g + 4],
                                        ring[:, g, :].rearrange("p (h k) -> p h k", h=4), AX.X, ALU.max)\
                            .then_inc(s["max_ok"], 1)
                    dve.wait_ge(s["g1_ps"], NT * n + t + 1)
                    v.tensor_reduce(mg[:, t, :], pa[t % 2][:, 0:NH * PRE].rearrange("p (h k) -> p h k", h=NH),
                                    AX.X, ALU.max).then_inc(s["gmax_ok"], 1)
                dve.wait_ge(s["gmax_ok"], NT * (n + 1))
                dve.wait_ge(s["max_ok"], 4 * NT * (n + 1))
                v.tensor_tensor(mt[:, :, :], m4[:, :, :], mg[:, :, :], ALU.max).then_inc(s["mt_ok"], 1)
                dve.wait_ge(s["mT_ps"], n + 1)
                if n >= 1:
                    dve.wait_ge(s["m_in"], 32 * n)
                    dve.wait_ge(s["pg_ps"], 2 * n)
                v.tensor_copy(mh[:, :], pa[0][0:NH, :]).then_inc(s["mhl"], 1)
                dve.wait_ge(s["mhl"], 2 * n + 1)
                v.tensor_tensor(ml[:, :], pa[0][0:NH, :], mh[:, :], ALU.subtract).then_inc(s["mhl"], 1)

            def Dd(n):
                if n + 1 < NS:
                    dve.wait_ge(s["kparts"], n + 2)
                for hf in range(2):
                    dve.wait_ge(s["pv_ok"], NC * n + 4 * (hf + 1))
                    if n >= 1:
                        dve.wait_ge(s["oT_ps"], NT * n)
                    v.tensor_copy(oS[:, hf, 0:2], pb[0][:, :].rearrange("p (g q) -> p g q", g=2))
                    v.tensor_copy(oS[:, hf, 2:4], pb[1][:, :].rearrange("p (g q) -> p g q", g=2))\
                        .then_inc(s["oS_ok"], 1)

            def Ee(n):
                for t in range(NT):
                    i = NT * n + t
                    dve.wait_ge(s["oT_ps"], i + 1)
                    o = pa[t % 2][:, :].rearrange("p (h e) -> p h e", e=32)
                    if i >= 2:
                        dve.wait_ge(s["otok_ok"], i - 1)
                        dve.wait_ge(s["o2_ps"], i - 1)
                    link(v.reciprocal(rden[:, i % 2, :], o[:, :, HD]))
                    v.tensor_tensor(otok[:, i % 2], o[:, :, 0:HD], rden[:, i % 2, :, None].broadcast_to((128, NH, HD)),
                                    ALU.mult).then_inc(s["otok_ok"], 1)
                for t in range(NT):
                    i = NT * n + t
                    dve.wait_ge(s["att_ps"], i + 1)
                    v.tensor_tensor(x_s[:, n, t, :], ring[:, t, D:2 * D], x_s[:, n, t, :], ALU.add)\
                        .then_inc(s["x1_ok"], 1)
                dve.wait_ge(s["x1_ok"], NT * (n + 1))
                stats(lambda t: x_s[:, n, t, :], n, "stats2")
                dve.wait_ge(s["rstd2_ok"], n + 1)
                dve.wait_ge(s["stats2"], n + 1)
                for t in range(NT):
                    v.tensor_scalar(xn2[:, t, :], x_s[:, n, t, :], mv[:, t, 0:1], rstd[:, t:t + 1],
                                    ALU.subtract, ALU.mult).then_inc(s["xn2_ok"], 1)

            def F(n):
                if n == 0:
                    dve.wait_ge(s["f_in"], 13 * 16)
                    link(v.tensor_scalar(nb1_s[:, :], b1_s[:, :], -1.0, None, ALU.mult))
                    v.tensor_tensor(b1d_s[:, :, :], b1_s[:, :, None].broadcast_to((128, NB, 24)),
                                    b1sel_s[:, :, :], ALU.mult).then_inc(s["b1d_ok"], 1)
                    dve.wait_ge(s["c_ps"], 1)
                    link(v.tensor_tensor(c24[:, :], pb[0][0:24, 0:D], b2_s[:, :], ALU.add))
                    link(v.tensor_copy(c24h[:, :], c24[:, :]))
                    link(v.tensor_tensor(c24r[:, :], c24[:, :], c24h[:, :], ALU.subtract))
                    link(v.tensor_copy(c24m[:, :], c24r[:, :]))
                    link(v.tensor_tensor(c24l[:, :], c24r[:, :], c24m[:, :], ALU.subtract))
                    link(v.tensor_scalar(c24t[:, :], c24h[:, :], psel_s[:, 0:1], None, ALU.mult))
                    link(v.scalar_tensor_tensor(c24r[:, :], c24m[:, :], psel_s[:, 1:2], c24t[:, :], ALU.mult, ALU.add))
                    v.scalar_tensor_tensor(cpart[:, :], c24l[:, :], psel_s[:, 2:3], c24r[:, :], ALU.mult, ALU.add)\
                        .then_inc(s["c_ok"], 1)
                    for e in range(E):
                        last = v.memset(iota_s[:, e:e + 1], float(E - e))
                    link(last)
                dve.wait_ge(s["lg_ps"], n + 1)
                if n >= 1:
                    dve.wait_ge(s["ohT_ps"], 2 * n)
                io = iota_s[:, None, :].broadcast_to((128, NT, E))
                link(v.tensor_tensor(lg[:, :, :], pa[1][:, 0:NT * E].rearrange("p (t e) -> p t e", t=NT),
                                     gb_s[:, None, :].broadcast_to((128, NT, E)), ALU.add))
                cur = lg

                def bc(a):
                    return a[:, :, None].broadcast_to((128, NT, E))

                for r in range(2):
                    link(v.tensor_reduce(top[:, :, r], cur[:, :, :], AX.X, ALU.max))
                    link(v.tensor_tensor(tmp8[:, :, :], cur[:, :, :], bc(top[:, :, r]), ALU.is_equal))
                    link(v.tensor_tensor(tmp8[:, :, :], tmp8[:, :, :], io, ALU.mult))
                    link(v.tensor_reduce(pk[:, :, r], tmp8[:, :, :], AX.X, ALU.max))
                    link(v.tensor_tensor(oh[:, r, :, 0, :], bc(pk[:, :, r]), io, ALU.is_equal))
                    link(v.tensor_copy(oh[:, r, :, 1, :], oh[:, r, :, 0, :]))
                    link(v.tensor_copy(oh[:, r, :, 2, :], oh[:, r, :, 0, :]))
                    if r == 0:
                        link(v.tensor_scalar(tmp8[:, :, :], oh[:, 0, :, 0, :], -3.0e38, None, ALU.mult))
                        link(v.tensor_tensor(lg2[:, :, :], lg[:, :, :], tmp8[:, :, :], ALU.add))
                        cur = lg2
                v.tensor_tensor(dif[:, :, 0:E], lg[:, :, :], bc(top[:, :, 0]), ALU.subtract)\
                    .then_inc(s["oh_ok"], 1)
                if n >= 1:
                    dve.wait_ge(s["ex_ok"], n)
                v.tensor_tensor(dif[:, :, E], top[:, :, 1], top[:, :, 0], ALU.subtract).then_inc(s["dif_ok"], 1)
                for r in range(2):
                    dve.wait_ge(s["ohT_ps"], 2 * n + r + 1)
                    v.tensor_copy(ohT[:, r, :], pa[r][0:24, :]).then_inc(s["ohT_ok"], 1)

                dve.wait_ge(s["ex_ok"], n + 1)
                link(v.tensor_reduce(dn[:, :], ex[:, :, 0:E], AX.X, ALU.add))
                link(v.reciprocal(rdn[:, :], dn[:, :]))
                v.tensor_copy(val[:, :, 0], rdn[:, :])
                link(v.tensor_tensor(val[:, :, 1], ex[:, :, E], rdn[:, :], ALU.mult))
                for r in range(2):
                    for j in range(NB):
                        i = (2 * n + r) * NB + j
                        dve.wait_ge(s["h_ps"], i + 1)
                        if j % 2 == 0:
                            dve.wait_ge(s["ohB_ok"], (2 * n + r) * E + j // 2 + 1)
                        if i >= 4:
                            dve.wait_ge(s["h_used"], i - 3)
                        v.scalar_tensor_tensor(hid[:, i % 4, :], ring[:, i % 4, :], nb1_s[:, j:j + 1],
                                               ohB[:, (i // 2) % 4, :], ALU.max, ALU.mult).then_inc(s["h_ok"], 1)
                    if r == 0:
                        dve.wait_ge(s["h_used"], NB * (2 * n + 1))
                        v.scalar_tensor_tensor(boost[:, :], pb[0][:, :], 0.5, xn2T[:, :], ALU.mult, ALU.add)\
                            .then_inc(s["boost_ok"], 1)
                if n >= 1:
                    dve.wait_ge(s["out_wr"], 16 * n)
                for r in range(2):
                    dve.wait_ge(s["yT_ps"], 2 * n + r + 1)
                    for t in range(NT):
                        last = v.scalar_tensor_tensor(z[:, t, :], pa[r][:, t * 128:(t + 1) * 128], val[:, t, r:r + 1],
                                                      (z if r else xn2)[:, t, :], ALU.mult, ALU.add)
                    last.then_inc(s["z_ok"], 1)
                    dve.wait_ge(s["z_ok"], 2 * n + r + 1)
                stats(lambda t: z[:, t, :], n, "stats3")
                dve.wait_ge(s["rstd3_ok"], n + 1)
                dve.wait_ge(s["stats3"], n + 1)
                for t in range(NT):
                    last = v.tensor_scalar(z[:, t, :], z[:, t, :], mv[:, t, 0:1], rstd[:, t:t + 1],
                                           ALU.subtract, ALU.mult)
                link(last)
                link(v.tensor_tensor(z[:, :, :], z[:, :, :], gam_s[:, None, :].broadcast_to((128, NT, D)), ALU.mult))
                link(v.tensor_tensor(z[:, :, :], z[:, :, :], bet_s[:, None, :].broadcast_to((128, NT, D)), ALU.add))
                v.tensor_tensor(z[:, :, :], z[:, :, :], x_s[:, n], ALU.add).then_inc(s["outs_ok"], 1)

            stage_order(A, C, Dd, Ee, F)


_WEIGHTS = ["L0_attn_x", "L0_attn_w_qkv", "L0_attn_w_out", "L0_ffn_gate_W", "L0_ffn_gate_b", "L0_ffn_W1",
            "L0_ffn_b1", "L0_ffn_W2", "L0_ffn_b2", "L0_ffn_ln_gamma", "L0_ffn_ln_beta"]


def _constants(np, bf16):
    D, NH, HD, W, PRE, ST, E, NB = 128, 16, 8, 64, 16, 512, 8, 16
    BIG = -(2.0 ** 100)
    col = np.arange(ST) % W
    row = np.arange(W)[:, None]
    kconst = np.zeros((128, 2, 8, 2, W), np.float32)
    kconst[W:, :, :, 0] = np.where(row.T <= row, BIG, 0.0)[:, None, None, :]
    kconst[W:, :, :, 1] = np.where(row.T > row, BIG, 0.0)[:, None, None, :]
    kconst[48, 0, 0, 0] = BIG
    kconst[48, 0, 0, 1, :PRE] = BIG
    kconst[48, 0, 1, 0, :PRE] = BIG
    kconst = kconst.reshape(128, 2, 2 * ST)
    kconst[49:51] = -1.0
    qconst = np.zeros((128, ST), np.float32)
    qconst[48] = 1.0
    qconst[W:] = (col[None, :] == row)
    maxsel = np.zeros((NH, 2, 128), np.float32)
    for h in range(NH):
        maxsel[h, h // 8, (h % 8) * PRE:(h % 8 + 1) * PRE] = -1.0
    q, k = np.arange(128)[:, None], np.arange(PRE)[None, :]
    after = np.where(k > q, BIG, 0.0).astype(np.float32)
    prefmask = np.tile(after, (1, NH))
    prefmaskT = np.tile(np.where(q < PRE, after, 0.0), (1, 8))
    p = np.arange(128)
    headsel = (p[:, None] // HD == np.arange(NH)[None, :]).astype(np.float32)
    selgrp = (p[:, None] // PRE == np.arange(NH)[None, :] % 8).astype(np.float32)
    b1sel = np.zeros((128, NB, 24), np.float32)
    for i in range(NB):
        b1sel[:, i, [i // 2, 8 + i // 2, 16 + i // 2]] = 1.0
    ohsel = np.zeros((24, E, 128), np.float32)
    for e in range(E):
        ohsel[e, e] = 1.0
    partsel = (np.arange(24)[:, None] // 8 == np.arange(3)[None, :]).astype(np.float32)
    ident = np.eye(128, dtype=np.float32)
    return {"ident": ident, "identb": ident.astype(bf16), "kconst": kconst.astype(bf16),
            "qconst": qconst.astype(bf16), "maxsel": maxsel.astype(bf16), "prefmask": prefmask.astype(bf16),
            "prefmaskT": prefmaskT.astype(bf16), "headsel": headsel, "selgrp": selgrp, "b1sel": b1sel,
            "ohsel": ohsel.astype(bf16), "partsel": partsel}


def kernel(**inputs):
    import numpy as np
    import ml_dtypes
    import concourse.bacc as bacc
    from concourse import mybir
    from concourse.bass_utils import run_bass_kernel_spmd

    a = {n: np.asarray(inputs[n]) for n in _WEIGHTS}
    x, wqkv, wo, gw, gb, w1, b1, w2, b2, gamma, beta = (a[n] for n in _WEIGHTS)
    arrays = {
        "x": x.reshape(2048, 128), "wqkvT": np.ascontiguousarray(wqkv.T), "woT": np.ascontiguousarray(wo.T),
        "gateW": gw, "gateb": gb, "W1": w1,
        "b1T": np.ascontiguousarray(b1.reshape(8, 2, 128).transpose(2, 0, 1).reshape(128, 16)),
        "W2": w2, "b2": b2, "gamma": gamma, "beta": beta,
    }
    arrays.update(_constants(np, ml_dtypes.bfloat16))
    nc = bacc.Bacc("TRN2", target_bir_lowering=False, num_devices=1)
    args = [nc.dram_tensor("in_" + n, v.shape, mybir.dt.from_np(v.dtype), kind="ExternalInput").ap()
            for n, v in arrays.items()]
    out = nc.dram_tensor("out_0", (2048, 128), mybir.dt.float32, kind="ExternalOutput").ap()
    preln_block_kernel(nc, *args, out)
    r = run_bass_kernel_spmd(nc, [{"in_" + n: np.ascontiguousarray(v) for n, v in arrays.items()}], core_ids=[0])
    return r.results[0]["out_0"].reshape(2, 1024, 128)
```

```python
import concourse.bass as bass
from concourse import mybir
from contextlib import ExitStack


def preln_block_kernel(nc, x, wqkvT, woT, gateW, gateb, W1, W2, bias, gamma, beta,
                       ident, identb, kconst, qconst, maxsel, prefmask, prefmaskT,
                       headsel, selgrp, upper, onesb, upto, steps, out):
    fp32 = mybir.dt.float32
    bf16 = mybir.dt.bfloat16
    i32 = mybir.dt.int32
    ALU = mybir.AluOpType
    ACT = mybir.ActivationFunctionType
    AX = mybir.AxisListType

    D = 128
    NH, HD = 16, 8
    SEQ = 1024
    W, PRE = 64, 16
    ST = 512
    NS = 4
    NT = ST // 128
    NC = ST // W
    NB = NS // 2
    BT = SEQ // 128
    E, HID = 8, 256
    NBLK = BT + E - 1
    CH = 5
    NCH = NBLK // CH
    NPROD = 6
    ROWS = NPROD * HD
    MROW = ROWS + 1
    NU = NT * 5
    EPS = 1e-5
    SCALE = float(HD) ** -0.5
    XM = 64

    QPUT = [(0, 0, 3, 1), (1, 3, 5, 1), (2, 5, 6, 1)]
    KPUT = [(0, 1, 6, 2), (1, 2, 5, 2), (2, 0, 1, 1)]

    qd = nc.dram_tensor("qstack", [NS, NPROD, HD, NH, ST], bf16).ap()
    kd = nc.dram_tensor("kstack", [NB, NPROD, HD, NH, SEQ], bf16).ap()
    xs = [nc.dram_tensor(f"slots_in{b}", [NBLK * 128, D], fp32).ap() for b in range(NB)]
    ys = [nc.dram_tensor(f"slots_out{i}", [NBLK * 128, D], fp32).ap() for i in range(2 * NB)]

    ctx = ExitStack()
    with ctx:
        def sb(name, shape, dt=fp32):
            return ctx.enter_context(nc.sbuf_tensor(name, shape, dt))

        def sem(name):
            return ctx.enter_context(nc.semaphore(name))

        wqkv_s = sb("wqkv_s", [128, 3 * D])
        wo_s = sb("wo_s", [128, D])
        gw_s = sb("gw_s", [128, E])
        gb_s = sb("gb_s", [128, E])
        w1_s = sb("w1_s", [128, 2, E * 128])
        w2_s = sb("w2_s", [128, 2, E * D])
        bias_s = sb("bias_s", [128, 24])
        bpart = sb("bpart", [3, 3, E * 128], bf16)
        bp = sb("bp", [128, 3, 24], bf16)
        br = sb("br", [128, 24])
        gam_s = sb("gam_s", [128, D])
        bet_s = sb("bet_s", [128, D])
        id_s = sb("id_s", [128, 128])
        idb_s = sb("idb_s", [128, 128], bf16)
        up_s = sb("up_s", [128, 128], bf16)
        ones_s = sb("ones_s", [128, 128], bf16)
        upto_s = sb("upto_s", [128, E, E])
        steps_s = sb("steps_s", [128, 16])
        msel_s = sb("msel_s", [NH, 2, 128], bf16)
        pm_s = sb("pm_s", [128, NH * PRE], bf16)
        pmT_s = sb("pmT_s", [128, 128], bf16)
        hsel_s = sb("hsel_s", [128, NH])
        gsel_s = sb("gsel_s", [128, NH])
        half_s = sb("half_s", [128, NT])
        zero_s = sb("zero_s", [128, D])
        zero_row = zero_s[:, :]
        x_s = sb("x_s", [128, NS, NT, D])
        st6 = sb("st6", [128, NT, 6])
        mv = sb("mv", [128, NT, 2])
        veps = sb("veps", [128, NT])
        rstd = sb("rstd", [128, NT])
        scr = sb("scr", [128, 2, ST])
        kr = scr[:, 0, :]
        qr = scr[:, 1, :]
        xn = scr[:, 1, :].rearrange("p (t d) -> p t d", t=NT)
        bst = scr[:, :, :].rearrange("p a t -> p (a t)").rearrange("p (t d) -> p t d", d=D)
        xnT = sb("xnT", [128, 2, XM + ST])
        kf = sb("kf", [128, ST])
        qf = sb("qf", [128, 2, ST])
        parts = sb("parts", [128, 2, 3, ST], bf16)
        kp = parts[:, 0]
        qp = parts[:, 1]
        yg = parts[:, :, :, :].rearrange("p a j t -> p (a j t)").bitcast(fp32)\
            .rearrange("p (t d) -> p t d", d=D)[:, 0:BT]
        xg = sb("xg", [128, 8, PRE])
        kg = sb("kg", [128, 2, NH, PRE])
        vg = sb("vg", [128, 2, 4, 4, 32])
        vaug = sb("vaug", [128, 2, 2, NT, NH, HD + 1])
        QS = sb("QS", [128, 2, NH, ST], bf16)
        KS = sb("KS", [128, 2, NH, NC, 2 * W], bf16)
        m4 = sb("m4", [128, NT, NH])
        mg = sb("mg", [128, NT, NH])
        mt = sb("mt", [128, NT, NH])
        mh = sb("mh", [NH, ST], bf16)
        ml = sb("ml", [NH, ST], bf16)
        pgx = sb("pgx", [128, 2 * CH * D])
        PG = pgx[:, 0:2 * ST].rearrange("p (g t) -> p g t", g=2)
        xin = pgx[:, :].rearrange("p (a j d) -> p a j d", a=2, j=CH)
        PT = sb("PT", [128, 2, NH, W])
        ptf = PT[:, :].rearrange("p a h q -> p (a h q)")
        early = ptf.bitcast(bf16)
        kc_s = early[:, 0:4 * ST].rearrange("p (a t) -> p a t", a=2)
        qc_s = early[:, 4 * ST:5 * ST]
        oS = sb("oS", [128, 2, 4, 256])
        rden = sb("rden", [128, 2, NH])
        otok = sb("otok", [128, 2, NH, HD])
        oT = sb("oT", [128, 2, D])
        xn2 = sb("xn2", [128, NS, NT, D])
        xn2T = kf
        lg = sb("lg", [128, NB, BT, E])
        lg2 = sb("lg2", [128, BT, E])
        tmp8 = sb("tmp8", [128, BT, E])
        pk = sb("pk", [128, BT, 2])
        top = sb("top", [128, 2, BT])
        oh = sb("oh", [128, BT, 2, E])
        ohb = sb("ohb", [128, BT, 2, E], bf16)
        dif = sb("dif", [128, BT, E + 1])
        ex = sb("ex", [128, BT, E + 1])
        dn = sb("dn", [128, BT])
        rdn = sb("rdn", [128, BT])
        val = sb("val", [128, NB, BT, 2])
        cnt = sb("cnt", [128, 2 * E])
        big = sb("big", [128, 2 * NBLK * E])
        cmp_ = big[:, 0:2 * E * BT].rearrange("p (c j) -> p c j", j=BT)
        pre = big[:, 0:2 * E * E].rearrange("p (r e f) -> p r e f", r=2, f=E)
        slot_of = big[:, 0:BT * 2 * E].rearrange("p (t c) -> p t c", t=BT)
        over = big[:, :].rearrange("p (r j e) -> p r j e", r=2, e=E)
        nblk = sb("nblk", [128, 2, E])
        endb = sb("endb", [128, 2, E])
        begb = sb("begb", [128, 2 * E])
        posf = sb("posf", [128, BT, 2])
        pos = sb("pos", [128, NB, BT, 2], i32)
        ebf = sb("ebf", [128, 2, NBLK])
        eb = sb("eb", [128, NB, 2, 16], i32)
        xT = oS[:, 0, 0, :].rearrange("p (a m) -> p a m", a=2)
        hs = oS[:, 0, 1:3, :]
        hT = oS[:, 1, 0:2, :]
        yb = ptf[:, 0:2 * CH * D].rearrange("p (a j d) -> p a j d", a=2, j=CH)

        pb = [ctx.enter_context(nc.psum_tensor(f"bank{i}", [128, 512], fp32)) for i in range(2)]
        ring = ctx.enter_context(nc.psum_tensor("ring", [128, 4, 512], fp32))
        pa = [ctx.enter_context(nc.psum_tensor(f"aux{i}", [128, 512], fp32)) for i in range(2)]

        names = """w_in x_in0 x_in1 x_in2 x_in3 c_in i_in f_in bp_ok bp_in st_init vones stats rstd_ok xn_ok
            xnT_ps xnT_ok k_ps q_ps v_ps vg_ps kf_ok qf_ok v_ok vg_ok kg_ok xg_ok kparts qparts kd_wr qd_wr
            ks_in0 ks_in1 qs_in0 qs_in1 s1_ps max_ok mt_ok mT_ps mhl m_in pg_ps pg_ok s2_ps pt_ok pv_ok oS_ok oT_ps otok_ok
            o2_ps oT_ok att_ps x1_ok stats2 rstd2_ok xn2_ok xn2T_ps xn2T_ok lg_ps lg_ok oh_ok dif_ok ex_ok
            pos_ps pos_ok eb_ok zs_ok zs_wr xs_wr0 xs_wr1 xs_wr2 xs_wr3 xin_in0 xin_in1 xT_ps xT_ok hm_ps hs_ok hT_ps hT_ok y_ps yb_ok ys_wr0 ys_wr1
            yga_in ygb_in bst_ok yg_used z_ok stats3 rstd3_ok outs_ok out_wr dchain pchain""".split()
        s = {n: sem(n) for n in names}
        block = ctx.enter_context(nc.Block())

        ORDER = ["L0", "A0", "L1", "A1", "L2", "C0", "D0", "A2", "E0", "L3", "D1", "A3", "E1", "D2", "E2",
                 "D3", "E3", "G1", "R0", "M0", "R1", "M1", "R2", "R3", "N0", "N1"]
        GATHERS = ["M0", "M1", "N0", "N1"]

        def run(**stages):
            for st in ORDER:
                if st[0] in stages:
                    stages[st[0]](int(st[1]))

        def psum_read(eng, st, aux_only=False):
            k, n = st[0], int(st[1])
            if k == "A":
                eng.wait_ge(s["v_ok"], 2 * (n + 1))
                eng.wait_ge(s["vg_ok"], 2 * (n // 2 + 1))
            if k == "C" or (k == "D" and n + 1 < NS):
                eng.wait_ge(s["mhl"], 2 * (n + 1) + (2 if k == "D" else 0))
            if k == "D" and not aux_only:
                eng.wait_ge(s["pt_ok"], NC * (n + 1))
                eng.wait_ge(s["oS_ok"], 4 * (n + 1))
            if k == "E":
                eng.wait_ge(s["x1_ok"], NT * (n + 1))
                eng.wait_ge(s["lg_ok"], n + 1)
            if k == "G":
                eng.wait_ge(s["pos_ok"], n + 1)
            if k == "R":
                for q in ("xT_ok", "hs_ok", "hT_ok", "yb_ok"):
                    eng.wait_ge(s[q], NBLK * (n + 1))

        def stage_before(st):
            i = ORDER.index(st) - 1
            while ORDER[i][0] in "LMN":
                i -= 1
            return ORDER[i]

        def done(kind, st):
            return sum(q[0] == kind for q in ORDER[:ORDER.index(st)])

        def rows_stored(eng, i):
            end = NCH * (i + 1)
            eng.wait_ge(s["ys_wr0"], 16 * ((end + 1) // 2))
            eng.wait_ge(s["ys_wr1"], 16 * (end // 2))

        def units_at(c):
            return range(NU * c // NC, NU * (c + 1) // NC)

        xv = x.rearrange("(s t p) d -> s p t d", t=NT, p=128)
        ov = out.rearrange("(s t p) d -> s p t d", t=NT, p=128)

        @block.sync
        def _(sp):
            sp.dma_start(x_s[:, 0], xv[0]).then_inc(s["x_in0"], 16)
            sp.dma_start(id_s[:, :], ident).then_inc(s["i_in"], 16)
            for dst, src in ((wqkv_s[:, :], wqkvT), (hsel_s[:, :], headsel), (gsel_s[:, :], selgrp),
                             (wo_s[:, :], woT), (bias_s[:, :], bias)):
                sp.dma_start(dst, src).then_inc(s["w_in"], 16)
            for n in range(1, NS):
                sp.dma_start(x_s[:, n], xv[n]).then_inc(s[f"x_in{n}"], 16)
            sp.wait_ge(s["st_init"], 2)

            def stacks(n):
                slot, b, c0 = n % 2, n // 2, (n % 2) * ST
                sp.wait_ge(s["kparts"], n + 1)
                for p, j0, j1, dj in KPUT:
                    for j in range(j0, j1, dj):
                        sp.dma_start(kd[b, j, :, :, c0:c0 + ST].rearrange("d h t -> h d t"), kp[:, p, :])\
                            .then_inc(s["kd_wr"], 16)
                sp.wait_ge(s["qparts"], n + 1)
                for p, j0, j1, dj in QPUT:
                    for j in range(j0, j1, dj):
                        sp.dma_start(qd[n, j].rearrange("d h t -> h d t"), qp[:, p, :]).then_inc(s["qd_wr"], 16)
                if n >= 2:
                    sp.wait_ge(s["s2_ps"], NC * (n - 1))
                sp.wait_ge(s["kd_wr"], 96 * (n + 1))
                kv = kd[b].rearrange("j d h t -> (j d) h t")
                for c in range(NC):
                    if c0 + c == 0:
                        src, dst = kv[:, :, 0:W], KS[0:ROWS, slot, :, c, W:2 * W]
                    else:
                        src, dst = kv[:, :, c0 + (c - 1) * W:c0 + (c + 1) * W], KS[0:ROWS, slot, :, c, :]
                    sp.dma_start(dst, src).then_inc(s[f"ks_in{slot}"], 16)
                sp.wait_ge(s["qd_wr"], 96 * (n + 1))
                sp.dma_start(QS[0:ROWS, slot, :, :], qd[n].rearrange("j d h t -> (j d) h t"))\
                    .then_inc(s[f"qs_in{slot}"], 16)
                sp.dma_start(QS[MROW:MROW + 2, slot, :, :],
                             qconst[MROW:MROW + 2, None, :].broadcast_to((2, NH, ST))).then_inc(s[f"qs_in{slot}"], 16)
                if n == 1:
                    sp.wait_ge(s["bp_ok"], 1)
                    for p in range(3):
                        sp.dma_start(bpart[p:p + 1, :, :].rearrange("o a c -> o (a c)"), bp[:, p, :])\
                            .then_inc(s["bp_in"], 16)
                    sp.wait_ge(s["zs_ok"], 1)
                    for b in range(NB):
                        sp.dma_start(xs[b].rearrange("(j p) d -> p j d", p=128),
                                     zero_s[:, None, :].broadcast_to((128, NBLK, D))).then_inc(s["zs_wr"], 16)

            def maxima(n):
                sp.wait_ge(s["mhl"], 2 * (n + 1))
                sp.dma_start(QS[MROW:MROW + 1, n % 2, :, :], mh[:, :]).then_inc(s["m_in"], 16)
                sp.dma_start(QS[MROW + 1:MROW + 2, n % 2, :, :], ml[:, :]).then_inc(s["m_in"], 16)

            def D_(n):
                if n + 1 < NS:
                    maxima(n + 1)

            def R_(i):
                for k in range(NCH):
                    K = NCH * i + k
                    sp.wait_ge(s[f"xs_wr{i}"], 16 * BT)
                    if K < 2:
                        sp.wait_ge(s["pv_ok"], NC * NS)
                    else:
                        sp.wait_ge(s["xT_ps"], CH * (K - 1))
                    sp.dma_start(xin[:, K % 2], xs[i % NB].rearrange("(k j p) d -> k p j d", j=CH, p=128)[k])\
                        .then_inc(s[f"xin_in{K % 2}"], 16)

            def N_(b):
                for n in (2 * b, 2 * b + 1):
                    sp.wait_ge(s["outs_ok"], n + 1)
                    sp.dma_start(ov[n], xn2[:, n]).then_inc(s["out_wr"], 16)

            run(A=stacks, C=maxima, D=D_, R=R_, N=N_)
            sp.wait_ge(s["out_wr"], 16 * NS)

        @block.gpsimd
        def _(pool):
            count = [0]

            def link(ins):
                count[0] += 1
                ins.then_inc(s["pchain"], 1)
                pool.wait_ge(s["pchain"], count[0])

            nc.gpsimd.memset(half_s[:, :], -0.5).then_inc(s["vones"], 1)
            nc.gpsimd.memset(xnT[:, 0, 0:XM], 0.0).then_inc(s["vones"], 1)
            nc.gpsimd.memset(zero_row, 0.0).then_inc(s["zs_ok"], 1)
            pool.wait_ge(s["vones"], 2)

            def inv_std(var_ok, n, done):
                pool.wait_ge(s[var_ok], n + 1)
                link(nc.gpsimd.tensor_scalar(veps[:, :], mv[:, :, 1], EPS, None, ALU.add))
                nc.gpsimd.tensor_tensor(rstd[:, :], veps[:, :], half_s[:, :], ALU.pow).then_inc(s[done], 1)

            def L_(n):
                inv_std("stats", n, "rstd_ok")
                if n == 0:
                    nc.gpsimd.memset(vg[:], 0.0).then_inc(s["vones"], 1)
                    nc.gpsimd.memset(vaug[:], 1.0).then_inc(s["vones"], 1)

            def A_(n):
                pool.wait_ge(s["qf_ok"], n + 1)
                if n >= 1:
                    pool.wait_ge(s["qd_wr"], 96 * n)
                q = qf[:, n % 2, :]
                link(nc.gpsimd.tensor_copy(qp[:, 0, :], q))
                link(nc.gpsimd.tensor_tensor(qr, q, qp[:, 0, :], ALU.subtract))
                link(nc.gpsimd.tensor_copy(qp[:, 1, :], qr))
                nc.gpsimd.tensor_tensor(qp[:, 2, :], qr, qp[:, 1, :], ALU.subtract)\
                    .then_inc(s["qparts"], 1)

            def E_(n):
                inv_std("stats2", n, "rstd2_ok")

            def scatter(b, r, t, rows):
                nc.gpsimd.indirect_dma_start(
                    out=xs[b], out_offset=bass.IndirectOffsetOnAxis(ap=pos[:, b, t, r:r + 1], axis=0),
                    in_=rows, in_offset=None).then_inc(s[f"xs_wr{NB * r + b}"], 16)

            def G_(b):
                pool.wait_ge(s["pos_ok"], b + 1)
                pool.wait_ge(s["zs_wr"], 16 * NB)
                for t in range(BT):
                    scatter(b, 0, t, xn2[:, 2 * b + t // NT, t % NT, :])

            def gathers(st, b, r):
                q = GATHERS.index(st)
                rows_stored(pool, NB * r + b)
                if q == 0:
                    pool.wait_ge(s["kd_wr"], 96 * NS)
                    pool.wait_ge(s["qd_wr"], 96 * NS)
                for t in range(BT):
                    if q >= 1 and t % NT == 0:
                        pool.wait_ge(s["yg_used"], 2 * (q - 1) + t // NT + 1)
                    nc.gpsimd.indirect_dma_start(
                        out=yg[:, t, :], out_offset=None, in_=ys[NB * r + b],
                        in_offset=bass.IndirectOffsetOnAxis(ap=pos[:, b, t, r:r + 1], axis=0))\
                        .then_inc(s["yga_in" if t < NT else "ygb_in"], 16)

            def M_(b):
                gathers(f"M{b}", b, 0)
                for t in range(BT):
                    if t % NT == 0:
                        pool.wait_ge(s["bst_ok"], 2 * b + t // NT + 1)
                    scatter(b, 1, t, bst[:, t, :])

            def N_(b):
                gathers(f"N{b}", b, 1)
                for n in (2 * b, 2 * b + 1):
                    inv_std("stats3", n, "rstd3_ok")

            def D_(n):
                if n == NS - 1:
                    G_(0)

            run(L=L_, A=A_, D=D_, E=E_, G=G_, M=M_, N=N_)

        @block.scalar
        def _(act):
            cs = [(kc_s[:, :, :], kconst), (qc_s[:, :], qconst), (idb_s[:, :], identb),
                  (pm_s[:, :], prefmask), (pmT_s[:, :], prefmaskT), (msel_s[:, :, :], maxsel)]
            for dst, src in cs:
                act.dma_start(dst, src).then_inc(s["c_in"], 16)
            fs = [(gw_s[:, :], gateW), (gb_s[:, :], gateb[None, :].broadcast_to((128, E))),
                  (up_s[:, :], upper), (ones_s[:, :], onesb), (upto_s[:, :, :], upto), (steps_s[:, :], steps),
                  (gam_s[:, :], gamma[None, :].broadcast_to((128, D))),
                  (bet_s[:, :], beta[None, :].broadcast_to((128, D)))]
            for a in range(2):
                fs.append((w1_s[:, a, :].rearrange("p (e c) -> p e c", e=E),
                           W1[:, :, a * 128:(a + 1) * 128].rearrange("e d c -> d e c")))
                fs.append((w2_s[:, a, :].rearrange("p (e c) -> p e c", e=E),
                           W2[:, a * 128:(a + 1) * 128, :].rearrange("e p d -> p e d")))

            def late_loads():
                for dst, src in fs:
                    act.dma_start(dst, src).then_inc(s["f_in"], 16)

            def A_(n):
                slot = n % 2
                act.wait_ge(s["xnT_ps"], n + 1)
                if n == 0:
                    act.wait_ge(s["vones"], 4)
                if n >= 2:
                    act.wait_ge(s["v_ps"], 2 * (n - 1))
                if slot == 0:
                    if n >= 2:
                        act.wait_ge(s["v_ps"], 2 * n)
                        act.wait_ge(s["xg_ok"], n // 2)
                    nc.scalar.copy(xnT[:, 1, 0:XM], pa[0][:, ST - XM:ST]).then_inc(s["xnT_ok"], 1)
                nc.scalar.copy(xnT[:, slot, XM:XM + ST], pa[0][:, :]).then_inc(s["xnT_ok"], 1)
                act.wait_ge(s["k_ps"], n + 1)
                if n >= 1:
                    act.wait_ge(s["kparts"], n)
                if done("E", f"A{n}"):
                    act.wait_ge(s["lg_ps"], done("E", f"A{n}"))
                nc.scalar.copy(kf[:, :], pa[1][:, :]).then_inc(s["kf_ok"], 1)
                act.wait_ge(s["q_ps"], n + 1)
                if n >= 2:
                    act.wait_ge(s["pg_ps"], 2 * (n - 1))
                    act.wait_ge(s["qparts"], n - 1)
                nc.scalar.mul(qf[:, slot, :], pa[0][:, :], SCALE).then_inc(s["qf_ok"], 1)
                if n >= 2:
                    act.wait_ge(s["pv_ok"], NC * (n - 1))
                for k in range(2):
                    act.wait_ge(s["v_ps"], 2 * n + k + 1)
                    nc.scalar.copy(vaug[:, slot, k, :, :, 0:HD],
                                   pa[1 - k][:, :].rearrange("p (t h d) -> p t h d", t=NT, d=HD))\
                        .then_inc(s["v_ok"], 1)
                if n == 0:
                    late_loads()

            def D_(n):
                for g in range(2):
                    act.wait_ge(s["pg_ps"], 2 * n + g + 1)
                    if n >= 1 and g == 0:
                        act.wait_ge(s["pv_ok"], NC * n)
                    nc.scalar.activation(PG[:, g, :], pa[g][:, :], ACT.Exp).then_inc(s["pg_ok"], 1)
                for c in range(NC):
                    i = NC * n + c
                    act.wait_ge(s["s2_ps"], i + 1)
                    if i >= 2:
                        act.wait_ge(s["pv_ok"], i - 1)
                    nc.scalar.activation(PT[:, i % 2].rearrange("p (g h) q -> p g (h q)", g=2),
                                         ring[:, 2 * (i % 2):2 * (i % 2) + 2, :], ACT.Exp)\
                        .then_inc(s["pt_ok"], 1)
                    if c % 4 == 0 and c > 0:
                        output(n, c // 4 - 1)
                        if n == NS - 1:
                            G_(0)
                output(n, 1)

            def output(n, hf):
                act.wait_ge(s["pv_ok"], NC * n + 4 * (hf + 1))
                if n >= 1 and hf == 0:
                    act.wait_ge(s["oT_ps"], NT * n)
                nc.scalar.copy(oS[:, hf, 0:2], pb[0][:, :].rearrange("p (g q) -> p g q", g=2))\
                    .then_inc(s["oS_ok"], 1)

            def E_(n):
                for t in range(NT):
                    i = NT * n + t
                    act.wait_ge(s["o2_ps"], i + 1)
                    if i >= 2:
                        act.wait_ge(s["att_ps"], i - 1)
                    nc.scalar.copy(oT[:, i % 2, :], ring[:, t, 0:D]).then_inc(s["oT_ok"], 1)
                act.wait_ge(s["xn2T_ps"], n + 1)
                if n >= 1:
                    act.wait_ge(s["lg_ps"], n)
                act.wait_ge(s["kparts"], done("A", f"E{n}"))
                nc.scalar.copy(xn2T[:, :], pa[0][:, :]).then_inc(s["xn2T_ok"], 1)

            def G_(b):
                act.wait_ge(s["dif_ok"], b + 1)
                nc.scalar.activation(ex[:, :, :], dif[:, :, :], ACT.Exp).then_inc(s["ex_ok"], 1)

            def R_(n):
                for st in range(NBLK + 3):
                    j, jy = st - 1, st - 3
                    if 0 <= j < NBLK:
                        i = NBLK * n + j
                        act.wait_ge(s["hm_ps"], i + 1)
                        if i >= 2:
                            act.wait_ge(s["hT_ps"], i - 1)
                        nc.scalar.activation(hs[:, i % 2, :], ring[:, i % 2, 0:HID], ACT.Relu)\
                            .then_inc(s["hs_ok"], 1)
                    if 0 <= jy < NBLK:
                        i = NBLK * n + jy
                        K = NCH * n + jy // CH
                        act.wait_ge(s["y_ps"], i + 1)
                        if K >= 2 and jy % CH == 0:
                            act.wait_ge(s[f"ys_wr{K % 2}"], 16 * (K // 2))
                        nc.scalar.copy(yb[:, K % 2, jy % CH, :], pb[i % 2][:, 0:D]).then_inc(s["yb_ok"], 1)
                        if jy % CH == CH - 1:
                            act.wait_ge(s["yb_ok"], CH * (K + 1))
                            act.dma_start(ys[n].rearrange("(k j p) d -> k p j d", j=CH, p=128)[K % NCH],
                                          yb[:, K % 2]).then_inc(s[f"ys_wr{K % 2}"], 16)

            run(A=A_, D=D_, E=E_, G=G_, R=R_)

        @block.tensor
        def _(pe):
            mm = nc.tensor.matmul

            def A_(n):
                slot = n % 2
                if n == 0:
                    pe.wait_ge(s["i_in"], 16)
                else:
                    psum_read(pe, stage_before(f"A{n}"), aux_only=True)
                pe.wait_ge(s["xn_ok"], NT * (n + 1))
                for t in range(NT):
                    last = nc.tensor.transpose(pa[0][:, t * 128:(t + 1) * 128], xn[:, t, :], id_s[:, :])
                last.then_inc(s["xnT_ps"], 1)
                pe.wait_ge(s["xnT_ok"], n + 1 + n // 2 + 1)
                if n == 0:
                    pe.wait_ge(s["w_in"], 5 * 16)
                xt = xnT[:, slot, XM:XM + ST]
                mm(pa[1][:, :], wqkv_s[:, D:2 * D], xt, start=True, stop=True).then_inc(s["k_ps"], 1)
                mm(pa[0][:, :], wqkv_s[:, 0:D], xt, start=True, stop=True).then_inc(s["q_ps"], 1)
                for k in range(2):
                    pe.wait_ge(s["kf_ok" if k == 0 else "qf_ok"], n + 1)
                    for t in range(NT):
                        c = t * 128 + (XM if k == 0 else 0)
                        last = mm(pa[1 - k][:, t * 128:(t + 1) * 128], xnT[:, slot, c:c + 128],
                                  wqkv_s[:, 2 * D:3 * D], start=True, stop=True)
                    last.then_inc(s["v_ps"], 1)
                if slot == 0:
                    pe.wait_ge(s["xg_ok"], n // 2 + 1)
                    pe.wait_ge(s["v_ok"], 2 * n + 1)
                    mm(pa[1][:, 0:D], xg[:, :, :].rearrange("p a k -> p (a k)"), wqkv_s[:, 2 * D:3 * D],
                       start=True, stop=True).then_inc(s["vg_ps"], 1)

            def unit(n, u):
                slot, b, t, g = n % 2, n // 2, u // 5, u % 5
                i = NU * n + u
                if i >= 2:
                    pe.wait_ge(s["max_ok"], i - 1)
                dst = pa[i % 2]
                if g < 4:
                    for hh in range(4):
                        for p in range(2):
                            c, h = 2 * t + p, 4 * g + hh
                            last = mm(dst[W * p:W * (p + 1), hh * 128:(hh + 1) * 128],
                                      QS[:, slot, h, c * W:(c + 1) * W], KS[:, slot, h, c, :],
                                      start=(hh == 0), stop=True, skip_group_check=True)
                else:
                    first = slot == 0 and t == 0
                    last = mm(dst[:, 0:NH * PRE], qf[:, slot, t * 128:(t + 1) * 128],
                              kg[:, b].rearrange("p h k -> p (h k)"), start=True, stop=not first)
                    if first:
                        last = mm(dst[:, 0:NH * PRE], idb_s[:, :], pm_s[:, :], start=False, stop=True)
                last.then_inc(s["s1_ps"], 1)

            def operands(n):
                if n == 0:
                    pe.wait_ge(s["c_in"], 96)
                    pe.wait_ge(s["st_init"], 2)
                pe.wait_ge(s[f"ks_in{n % 2}"], 16 * NC * (n // 2 + 1))
                pe.wait_ge(s[f"qs_in{n % 2}"], 32 * (n // 2 + 1))
                pe.wait_ge(s["kg_ok"], n // 2 + 1)

            def turn_maxima(n):
                pe.wait_ge(s["mt_ok"], n + 1)
                for t in range(NT):
                    last = nc.tensor.transpose(pa[0][0:NH, t * 128:(t + 1) * 128], mt[:, t, :], id_s[:, :])
                last.then_inc(s["mT_ps"], 1)

            def C_(n):
                psum_read(pe, stage_before(f"C{n}"))
                operands(n)
                for u in range(NU):
                    unit(n, u)
                turn_maxima(n)

            def D_(n):
                slot, b = n % 2, n // 2
                psum_read(pe, stage_before(f"D{n}"))
                pe.wait_ge(s["mhl"], 2 * (n + 1))
                pe.wait_ge(s["vg_ok"], 2 * (b + 1))
                pe.wait_ge(s["v_ok"], 2 * (n + 1))
                for g in range(2):
                    mm(pa[g][:, :], kg[:, b, 8 * g:8 * g + 8].rearrange("p h k -> p (h k)"), qf[:, slot, :],
                       start=True, stop=False)
                    mm(pa[g][:, :], msel_s[:, g, :], mh[:, :], start=False, stop=False)
                    if slot == 0:
                        mm(pa[g][:, 0:PRE], pmT_s[:, :], idb_s[:, 0:PRE], start=False, stop=False)
                    mm(pa[g][:, :], msel_s[:, g, :], ml[:, :], start=False, stop=True).then_inc(s["pg_ps"], 1)
                pe.wait_ge(s["m_in"], 32 * (n + 1))

                def scores(c):
                    i = NC * n + c
                    if i >= 2:
                        pe.wait_ge(s["pt_ok"], i - 1)
                    for h in range(NH):
                        last = mm(ring[:, 2 * (i % 2) + h // 8, (h % 8) * W:(h % 8 + 1) * W],
                                  KS[:, slot, h, c, :], QS[:, slot, h, c * W:(c + 1) * W],
                                  start=(h % 8 == 0), stop=True, skip_group_check=True)
                    last.then_inc(s["s2_ps"], 1)

                def values(c):
                    i = NC * n + c
                    pe.wait_ge(s["pt_ok"], i + 1)
                    if c % 4 == 0:
                        if i >= 4:
                            pe.wait_ge(s["oS_ok"], i // 2)
                        for g in range(4):
                            mm(pb[g // 2][:, (g % 2) * 256:(g % 2 + 1) * 256],
                               vg[:, b, g].rearrange("p i e -> p (i e)"),
                               PG[:, g // 2, (c // 4) * 256:(c // 4 + 1) * 256],
                               start=(g % 2 == 0), stop=True, skip_group_check=True)
                    for h in range(NH):
                        g, q = h // 4, h % 4
                        col = (g % 2) * 256 + (c % 4) * W
                        last = mm(pb[g // 2][32 * q:32 * q + HD + 1, col:col + W],
                                  vaug[:, slot, 0 if c % 2 else 1, c // 2, h, :], PT[:, i % 2, h, :],
                                  start=False, stop=True, skip_group_check=True)
                    last.then_inc(s["pv_ok"], 1)

                scores(0)
                pe.wait_ge(s["pg_ok"], 2 * (n + 1))
                if n + 1 < NS:
                    operands(n + 1)
                for c in range(NC):
                    if c + 1 < NC:
                        scores(c + 1)
                    if n + 1 < NS:
                        for u in units_at(c):
                            unit(n + 1, u)
                    values(c)
                    if n == NS - 1 and c == 3:
                        G_(0)
                if n + 1 < NS:
                    turn_maxima(n + 1)

            def E_(n):
                psum_read(pe, f"D{n}")
                if stage_before(f"E{n}") != f"D{n}":
                    psum_read(pe, stage_before(f"E{n}"))
                for t in range(NT):
                    i = NT * n + t
                    if t >= 2:
                        pe.wait_ge(s["otok_ok"], i - 1)
                    for g in range(4):
                        last = nc.tensor.transpose(pa[t % 2][:, g * 128:(g + 1) * 128],
                                                   oS[:, t // 2, g, (t % 2) * 128:(t % 2 + 1) * 128], id_s[:, :])
                    last.then_inc(s["oT_ps"], 1)
                    if t >= 1:
                        back(i - 1)
                    if t >= 2:
                        project(i - 2)
                back(NT * n + 3)
                project(NT * n + 2)
                project(NT * n + 3)
                pe.wait_ge(s["xn2_ok"], NT * (n + 1))
                for t in range(NT):
                    last = nc.tensor.transpose(pa[0][:, t * 128:(t + 1) * 128], xn2[:, n, t, :], id_s[:, :])
                last.then_inc(s["xn2T_ps"], 1)
                pe.wait_ge(s["xn2T_ok"], n + 1)
                if n == 0:
                    pe.wait_ge(s["f_in"], 12 * 16)
                for t in range(NT):
                    last = mm(pa[1][:, t * E:(t + 1) * E], xn2T[:, t * 128:(t + 1) * 128], gw_s[:, :],
                              start=True, stop=True)
                last.then_inc(s["lg_ps"], 1)

            def back(i):
                pe.wait_ge(s["otok_ok"], i + 1)
                nc.tensor.transpose(ring[:, i % 4, 0:D], otok[:, i % 2].rearrange("p h d -> p (h d)"), id_s[:, :])\
                    .then_inc(s["o2_ps"], 1)

            def project(i):
                pe.wait_ge(s["oT_ok"], i + 1)
                mm(ring[:, i % 4, D:2 * D], oT[:, i % 2, :], wo_s[:, :], start=True, stop=True)\
                    .then_inc(s["att_ps"], 1)

            def G_(b):
                if b == 1:
                    psum_read(pe, "E3")
                pe.wait_ge(s["oh_ok"], b + 1)
                def row(t):
                    return ohb[:, t].rearrange("p r e -> p (r e)")

                C = 2 * E
                mm(pa[0][:, 0:BT * C], up_s[:, :], ohb[:, :, :, :].rearrange("p t r e -> p (t r e)"),
                   start=True, stop=True, skip_group_check=True)
                for t in range(BT - 1):
                    mm(pa[0][:, (t + 1) * C:BT * C].rearrange("p (t c) -> p t c", c=C), ones_s[:, :],
                       row(t)[:, None, :].broadcast_to((128, BT - 1 - t, C)),
                       start=False, stop=True, skip_group_check=True)
                for t in range(BT):
                    last = mm(pa[1][:, 0:C], ones_s[:, :], row(t), start=(t == 0), stop=(t == BT - 1))
                last.then_inc(s["pos_ps"], 1)

            def R_(n):
                psum_read(pe, stage_before(f"R{n}"))
                r, b = n // NB, n % NB
                pe.wait_ge(s["eb_ok"], b + 1)
                if n == 0:
                    pe.wait_ge(s["bp_in"], 48)
                _, off = nc.values_load_multi_w_load_instructions(
                    eb[0:1, b, r, 0:NBLK], engines=[mybir.EngineType.PE], min_val=0, max_val=(E - 1) * 128,
                    skip_runtime_bounds_check_because="the kernel clips the expert to the last one")
                for st in range(NBLK + 3):
                    if st < NBLK:
                        i = NBLK * n + st
                        K = NCH * n + st // CH
                        if st % CH == 0:
                            pe.wait_ge(s[f"xin_in{K % 2}"], 16 * (K // 2 + 1))
                        if i >= 2:
                            pe.wait_ge(s["xT_ok"], i - 1)
                        nc.tensor.transpose(pa[i % 2][:, 0:128], xin[:, K % 2, st % CH, :], id_s[:, :])\
                            .then_inc(s["xT_ps"], 1)
                    if 0 <= st - 1 < NBLK:
                        i, o = NBLK * n + st - 1, off[st - 1]
                        pe.wait_ge(s["xT_ok"], i + 1)
                        if i >= 2:
                            pe.wait_ge(s["hs_ok"], i - 1)
                        dst = ring[:, i % 2, 0:HID].rearrange("p (a c) -> p a c", a=2)
                        mm(dst, xT[:, i % 2, :], w1_s[:, :, bass.ds(o, 128)], start=True, stop=False)
                        mm(dst, ones_s[0:3, :], bpart[0:3, 0:2, bass.ds(o, 128)], start=False, stop=True)\
                            .then_inc(s["hm_ps"], 1)
                    if 0 <= st - 2 < NBLK:
                        i = NBLK * n + st - 2
                        pe.wait_ge(s["hs_ok"], i + 1)
                        if i >= 2:
                            pe.wait_ge(s["hT_ok"], i - 1)
                        for a in range(2):
                            last = nc.tensor.transpose(ring[:, 2 + i % 2, a * 128:(a + 1) * 128],
                                                       hs[:, i % 2, a * 128:(a + 1) * 128], id_s[:, :])
                        last.then_inc(s["hT_ps"], 1)
                    if 0 <= st - 3 < NBLK:
                        i, o = NBLK * n + st - 3, off[st - 3]
                        pe.wait_ge(s["hT_ok"], i + 1)
                        if i >= 2:
                            pe.wait_ge(s["yb_ok"], i - 1)
                        for a in range(2):
                            mm(pb[i % 2][:, 0:D], hT[:, i % 2, a * 128:(a + 1) * 128],
                               w2_s[:, a, bass.ds(o, 128)], start=(a == 0), stop=False)
                        mm(pb[i % 2][:, 0:D], ones_s[0:3, :], bpart[0:3, 2, bass.ds(o, 128)],
                           start=False, stop=True).then_inc(s["y_ps"], 1)

            run(A=A_, C=C_, D=D_, E=E_, G=G_, R=R_)

        @block.vector
        def _(dve):
            v = nc.vector
            count = [0]

            def link(ins):
                count[0] += 1
                ins.then_inc(s["dchain"], 1)
                dve.wait_ge(s["dchain"], count[0])

            normed = []

            def stats(src, n, var_ok):
                for name, value in normed:
                    dve.wait_ge(s[name], value)
                for t in range(NT):
                    last = v.bn_stats(st6[:, t, :], src(t))
                link(last)
                for t in range(NT):
                    last = v.bn_aggr(mv[:, t, :], st6[:, t, :])
                last.then_inc(s[var_ok], 1)

            def L_(n):
                if n >= 1:
                    dve.wait_ge(s["xnT_ps"], n)
                    dve.wait_ge(s["qparts"], n)
                dve.wait_ge(s[f"x_in{n}"], 16)
                stats(lambda t: x_s[:, n, t, :], n, "stats")
                dve.wait_ge(s["rstd_ok"], n + 1)
                dve.wait_ge(s["stats"], n + 1)
                for t in range(NT):
                    v.tensor_scalar(xn[:, t, :], x_s[:, n, t, :], mv[:, t, 0:1], rstd[:, t:t + 1],
                                    ALU.subtract, ALU.mult).then_inc(s["xn_ok"], 1)
                normed[:] = [("xn_ok", NT * (n + 1))]

            def A_(n):
                if n == 0:
                    dve.wait_ge(s["c_in"], 96)
                    for slot in range(2):
                        v.tensor_copy(KS[:, slot].rearrange("p h c k -> p h (c k)"),
                                      kc_s[:, None, slot, :].broadcast_to((128, NH, 2 * ST)))
                        last = v.tensor_copy(QS[:, slot, :, :], qc_s[:, None, :].broadcast_to((128, NH, ST)))
                        last.then_inc(s["st_init"], 1)
                if n % 2 == 0:
                    dve.wait_ge(s["xnT_ok"], n + 1 + n // 2 + 1)
                    if n >= 2:
                        dve.wait_ge(s["vg_ps"], n // 2)
                    v.tensor_copy(xg[:, :, :], xnT[:, 0, None, XM:XM + PRE].broadcast_to((128, 8, PRE)))\
                        .then_inc(s["xg_ok"], 1)
                dve.wait_ge(s["kf_ok"], n + 1)
                if n % 2 == 0:
                    if n == 0:
                        dve.wait_ge(s["w_in"], 5 * 16)
                    v.tensor_tensor(kg[:, n // 2], kf[:, None, 0:PRE].broadcast_to((128, NH, PRE)),
                                    hsel_s[:, :, None].broadcast_to((128, NH, PRE)), ALU.mult)\
                        .then_inc(s["kg_ok"], 1)
                if n >= 1:
                    dve.wait_ge(s["kd_wr"], 96 * n)
                link(v.tensor_copy(kp[:, 0, :], kf[:, :]))
                link(v.tensor_tensor(kr, kf[:, :], kp[:, 0, :], ALU.subtract))
                link(v.tensor_copy(kp[:, 1, :], kr))
                v.tensor_tensor(kp[:, 2, :], kr, kp[:, 1, :], ALU.subtract).then_inc(s["kparts"], 1)
                if n % 2 == 0:
                    b = n // 2
                    dve.wait_ge(s["vg_ps"], b + 1)
                    dve.wait_ge(s["vones"], 4)
                    v.tensor_tensor(vg[:, b, :, :, 0:HD].rearrange("p g i d -> p (g i) d"),
                                    pa[1][:, 0:D].rearrange("p (h d) -> p h d", d=HD),
                                    gsel_s[:, :, None].broadcast_to((128, NH, HD)), ALU.mult)\
                        .then_inc(s["vg_ok"], 1)
                    v.tensor_copy(vg[:, b, :, :, HD].rearrange("p g i -> p (g i)"), gsel_s[:, :])\
                        .then_inc(s["vg_ok"], 1)
                if n == 1:
                    link(v.tensor_copy(bp[:, 0, :], bias_s[:, :]))
                    link(v.tensor_tensor(br[:, :], bias_s[:, :], bp[:, 0, :], ALU.subtract))
                    link(v.tensor_copy(bp[:, 1, :], br[:, :]))
                    v.tensor_tensor(bp[:, 2, :], br[:, :], bp[:, 1, :], ALU.subtract).then_inc(s["bp_ok"], 1)

            def unit_max(n, u):
                t, g = u // 5, u % 5
                i = NU * n + u
                dve.wait_ge(s["s1_ps"], i + 1)
                if g < 4:
                    v.tensor_reduce(m4[:, t, 4 * g:4 * g + 4], pa[i % 2][:, :].rearrange("p (h k) -> p h k", h=4),
                                    AX.X, ALU.max).then_inc(s["max_ok"], 1)
                else:
                    v.tensor_reduce(mg[:, t, :], pa[i % 2][:, 0:NH * PRE].rearrange("p (h k) -> p h k", h=NH),
                                    AX.X, ALU.max).then_inc(s["max_ok"], 1)

            def maxima(n):
                dve.wait_ge(s["max_ok"], NU * (n + 1))
                v.tensor_tensor(mt[:, :, :], m4[:, :, :], mg[:, :, :], ALU.max).then_inc(s["mt_ok"], 1)
                dve.wait_ge(s["mT_ps"], n + 1)
                if n >= 1:
                    dve.wait_ge(s["m_in"], 32 * n)
                    dve.wait_ge(s["pg_ps"], 2 * n)
                v.tensor_copy(mh[:, :], pa[0][0:NH, :]).then_inc(s["mhl"], 1)
                dve.wait_ge(s["mhl"], 2 * n + 1)
                v.tensor_tensor(ml[:, :], pa[0][0:NH, :], mh[:, :], ALU.subtract).then_inc(s["mhl"], 1)

            def C_(n):
                for u in range(NU):
                    unit_max(n, u)
                maxima(n)

            def D_(n):
                if n >= 1:
                    dve.wait_ge(s["mt_ok"], n)
                if n == NS - 1:
                    select(0)
                for c in range(NC):
                    if n + 1 < NS:
                        for u in units_at(c):
                            unit_max(n + 1, u)
                    if c % 4 == 3:
                        hf = c // 4
                        dve.wait_ge(s["pv_ok"], NC * n + 4 * (hf + 1))
                        if n >= 1:
                            dve.wait_ge(s["oT_ps"], NT * n)
                        v.tensor_copy(oS[:, hf, 2:4], pb[1][:, :].rearrange("p (g q) -> p g q", g=2))\
                            .then_inc(s["oS_ok"], 1)
                        if n == NS - 1 and hf == 0:
                            place(0)
                if n + 1 < NS:
                    maxima(n + 1)

            def E_(n):
                for t in range(NT):
                    i = NT * n + t
                    dve.wait_ge(s["oT_ps"], i + 1)
                    o = pa[t % 2][:, :].rearrange("p (h e) -> p h e", e=32)
                    if i >= 2:
                        dve.wait_ge(s["otok_ok"], i - 1)
                        dve.wait_ge(s["o2_ps"], i - 1)
                    link(v.reciprocal(rden[:, i % 2, :], o[:, :, HD]))
                    v.tensor_tensor(otok[:, i % 2], o[:, :, 0:HD], rden[:, i % 2, :, None].broadcast_to((128, NH, HD)),
                                    ALU.mult).then_inc(s["otok_ok"], 1)
                for t in range(NT):
                    i = NT * n + t
                    dve.wait_ge(s["att_ps"], i + 1)
                    v.tensor_tensor(x_s[:, n, t, :], ring[:, t, D:2 * D], x_s[:, n, t, :], ALU.add)\
                        .then_inc(s["x1_ok"], 1)
                dve.wait_ge(s["x1_ok"], NT * (n + 1))
                stats(lambda t: x_s[:, n, t, :], n, "stats2")
                dve.wait_ge(s["rstd2_ok"], n + 1)
                dve.wait_ge(s["stats2"], n + 1)
                for t in range(NT):
                    v.tensor_scalar(xn2[:, n, t, :], x_s[:, n, t, :], mv[:, t, 0:1], rstd[:, t:t + 1],
                                    ALU.subtract, ALU.mult).then_inc(s["xn2_ok"], 1)
                normed[:] = [("xn2_ok", NT * (n + 1))]
                if n == 0:
                    dve.wait_ge(s["f_in"], 12 * 16)
                dve.wait_ge(s["lg_ps"], n + 1)
                v.tensor_tensor(lg[:, n // 2, (n % 2) * NT:(n % 2 + 1) * NT, :],
                                pa[1][:, 0:NT * E].rearrange("p (t e) -> p t e", t=NT),
                                gb_s[:, None, :].broadcast_to((128, NT, E)), ALU.add).then_inc(s["lg_ok"], 1)

            def select(b):
                dve.wait_ge(s["lg_ok"], 2 * (b + 1))
                io = steps_s[:, None, 0:E].broadcast_to((128, BT, E))

                def bc(a):
                    return a[:, :, None].broadcast_to((128, BT, E))

                cur = lg[:, b]
                for r in range(2):
                    link(v.tensor_reduce(top[:, r, :], cur, AX.X, ALU.max))
                    link(v.tensor_tensor(tmp8[:, :, :], cur, bc(top[:, r, :]), ALU.is_lt))
                    link(v.scalar_tensor_tensor(tmp8[:, :, :], tmp8[:, :, :], 16.0, io, ALU.mult, ALU.add))
                    link(v.tensor_reduce(pk[:, :, r], tmp8[:, :, :], AX.X, ALU.min))
                    link(v.tensor_tensor(oh[:, :, r, :], bc(pk[:, :, r]), io, ALU.is_equal))
                    if r == 0:
                        link(v.scalar_tensor_tensor(lg2[:, :, :], oh[:, :, 0, :], -3.0e38, lg[:, b],
                                                    ALU.mult, ALU.add))
                        cur = lg2[:, :, :]
                v.tensor_copy(ohb[:, :, :, :], oh[:, :, :, :]).then_inc(s["oh_ok"], 1)
                v.tensor_tensor(dif[:, :, 0:E], lg[:, b], bc(top[:, 0, :]), ALU.subtract)
                v.tensor_tensor(dif[:, :, E], top[:, 1, :], top[:, 0, :], ALU.subtract).then_inc(s["dif_ok"], 1)

            def place(b):
                dve.wait_ge(s["pos_ps"], b + 1)
                link(v.tensor_copy(cnt[:, :], pa[1][:, 0:2 * E]))
                link(v.scalar_tensor_tensor(cmp_, steps_s[:, None, 0:BT].broadcast_to((128, 2 * E, BT)), 128.0,
                                            cnt[:, :, None].broadcast_to((128, 2 * E, BT)), ALU.mult, ALU.is_lt))
                link(v.tensor_reduce(nblk[:, :, :].rearrange("p r e -> p (r e)"), cmp_, AX.X, ALU.add))
                for r in range(2):
                    last = v.tensor_tensor(pre[:, r], nblk[:, r, None, :].broadcast_to((128, E, E)),
                                           upto_s[:, :, :], ALU.mult)
                link(last)
                link(v.tensor_reduce(endb[:, :, :], pre, AX.X, ALU.add))
                link(v.tensor_tensor(begb[:, :], endb[:, :, :].rearrange("p r e -> p (r e)"),
                                     nblk[:, :, :].rearrange("p r e -> p (r e)"), ALU.subtract))
                link(v.scalar_tensor_tensor(slot_of, begb[:, None, :].broadcast_to((128, BT, 2 * E)), 128.0,
                                            pa[0][:, 0:BT * 2 * E].rearrange("p (t c) -> p t c", t=BT),
                                            ALU.mult, ALU.add))
                link(v.tensor_tensor(slot_of, slot_of, oh[:, :, :, :].rearrange("p t r e -> p t (r e)"), ALU.mult))
                link(v.tensor_reduce(posf[:, :, :], slot_of.rearrange("p t (r e) -> p t r e", r=2), AX.X, ALU.add))
                v.tensor_copy(pos[:, b], posf[:, :, :]).then_inc(s["pos_ok"], 1)
                for r in range(2):
                    last = v.tensor_tensor(over[:, r], endb[:, r, None, :].broadcast_to((128, NBLK, E)),
                                           steps_s[:, 0:NBLK, None].broadcast_to((128, NBLK, E)), ALU.is_le)
                link(last)
                link(v.tensor_reduce(ebf[:, :, :], over, AX.X, ALU.add))
                v.tensor_scalar(eb[:, b, :, 0:NBLK], ebf[:, :, :], float(E - 1), 128.0, ALU.min, ALU.mult)\
                    .then_inc(s["eb_ok"], 1)
                dve.wait_ge(s["ex_ok"], b + 1)
                link(v.tensor_reduce(dn[:, :], ex[:, :, 0:E], AX.X, ALU.add))
                link(v.reciprocal(rdn[:, :], dn[:, :]))
                v.tensor_copy(val[:, b, :, 0], rdn[:, :])
                link(v.tensor_tensor(val[:, b, :, 1], ex[:, :, E], rdn[:, :], ALU.mult))

            def G_(b):
                select(b)
                place(b)

            def R_(n):
                for st in range(NBLK + 2):
                    if st < NBLK:
                        i = NBLK * n + st
                        dve.wait_ge(s["xT_ps"], i + 1)
                        if i >= 2:
                            dve.wait_ge(s["hm_ps"], i - 1)
                        v.tensor_copy(xT[:, i % 2, :], pa[i % 2][:, 0:128]).then_inc(s["xT_ok"], 1)
                    if st >= 2:
                        i = NBLK * n + st - 2
                        dve.wait_ge(s["hT_ps"], i + 1)
                        if i >= 2:
                            dve.wait_ge(s["y_ps"], i - 1)
                        v.tensor_copy(hT[:, i % 2, :], ring[:, 2 + i % 2, 0:HID]).then_inc(s["hT_ok"], 1)
                    if n in (1, 2) and st in (8, 10):
                        boost(n - 1, (st - 8) // 2)
                    if n in (1, 2) and st in (12, 14):
                        weigh_first(n - 1, (st - 12) // 2)
                    if n == 3 and st in (8, 12):
                        finish(0, (st - 8) // 4)

            def rows_in(q, hf):
                dve.wait_ge(s["yga_in" if hf == 0 else "ygb_in"], 16 * NT * (q + 1))

            def weigh(b, r, hf):
                for t in range(NT):
                    k = hf * NT + t
                    last = v.scalar_tensor_tensor(xn2[:, 2 * b + hf, t, :], yg[:, k, :], val[:, b, k, r:r + 1],
                                                  xn2[:, 2 * b + hf, t, :], ALU.mult, ALU.add)
                return last

            def boost(b, hf):
                rows_in(GATHERS.index(f"M{b}"), hf)
                if b == 1:
                    dve.wait_ge(s["xs_wr2"], 16 * BT)
                v.scalar_tensor_tensor(bst[:, hf * NT:(hf + 1) * NT, :], yg[:, hf * NT:(hf + 1) * NT, :], 0.5,
                                       xn2[:, 2 * b + hf], ALU.mult, ALU.add).then_inc(s["bst_ok"], 1)

            def weigh_first(b, hf):
                dve.wait_ge(s["bst_ok"], 2 * b + hf + 1)
                weigh(b, 0, hf).then_inc(s["yg_used"], 1)

            def finish(b, hf):
                q, n = GATHERS.index(f"N{b}"), 2 * b + hf
                rows_in(q, hf)
                dve.wait_ge(s["yg_used"], 2 * q + hf)
                weigh(b, 1, hf).then_inc(s["yg_used"], 1)
                dve.wait_ge(s["yg_used"], 2 * q + hf + 1)
                z = xn2[:, n]
                stats(lambda t: z[:, t, :], n, "stats3")
                dve.wait_ge(s["rstd3_ok"], n + 1)
                dve.wait_ge(s["stats3"], n + 1)
                for t in range(NT):
                    last = v.tensor_scalar(z[:, t, :], z[:, t, :], mv[:, t, 0:1], rstd[:, t:t + 1],
                                           ALU.subtract, ALU.mult)
                link(last)
                link(v.tensor_tensor(z, z, gam_s[:, None, :].broadcast_to((128, NT, D)), ALU.mult))
                link(v.tensor_tensor(z, z, bet_s[:, None, :].broadcast_to((128, NT, D)), ALU.add))
                v.tensor_tensor(z, z, x_s[:, n], ALU.add).then_inc(s["outs_ok"], 1)
                normed[:] = [("outs_ok", n + 1)]

            def N_(b):
                if b == 1:
                    finish(1, 0)
                    finish(1, 1)

            run(L=L_, A=A_, C=C_, D=D_, E=E_, G=G_, R=R_, N=N_)


_WEIGHTS = ["L0_attn_x", "L0_attn_w_qkv", "L0_attn_w_out", "L0_ffn_gate_W", "L0_ffn_gate_b", "L0_ffn_W1",
            "L0_ffn_b1", "L0_ffn_W2", "L0_ffn_b2", "L0_ffn_ln_gamma", "L0_ffn_ln_beta"]


def _constants(np, bf16):
    D, NH, HD, W, PRE, ST, E = 128, 16, 8, 64, 16, 512, 8
    BIG = -(2.0 ** 100)
    col = np.arange(ST) % W
    row = np.arange(W)[:, None]
    kconst = np.zeros((128, 2, 8, 2, W), np.float32)
    kconst[W:, :, :, 0] = np.where(row.T <= row, BIG, 0.0)[:, None, None, :]
    kconst[W:, :, :, 1] = np.where(row.T > row, BIG, 0.0)[:, None, None, :]
    kconst[48, 0, 0, 0] = BIG
    kconst[48, 0, 0, 1, :PRE] = BIG
    kconst[48, 0, 1, 0, :PRE] = BIG
    kconst = kconst.reshape(128, 2, 2 * ST)
    kconst[49:51] = -1.0
    qconst = np.zeros((128, ST), np.float32)
    qconst[48] = 1.0
    qconst[W:] = (col[None, :] == row)
    maxsel = np.zeros((NH, 2, 128), np.float32)
    for h in range(NH):
        maxsel[h, h // 8, (h % 8) * PRE:(h % 8 + 1) * PRE] = -1.0
    q, k = np.arange(128)[:, None], np.arange(PRE)[None, :]
    after = np.where(k > q, BIG, 0.0).astype(np.float32)
    prefmask = np.tile(after, (1, NH))
    prefmaskT = np.tile(np.where(q < PRE, after, 0.0), (1, 8))
    p = np.arange(128)
    headsel = (p[:, None] // HD == np.arange(NH)[None, :]).astype(np.float32)
    selgrp = (p[:, None] // PRE == np.arange(NH)[None, :] % 8).astype(np.float32)
    upper = (p[:, None] < p[None, :]).astype(np.float32)
    upto = np.broadcast_to(np.arange(E)[None, :] <= np.arange(E)[:, None], (128, E, E)).astype(np.float32)
    steps = np.broadcast_to(np.arange(16), (128, 16)).astype(np.float32)
    ident = np.eye(128, dtype=np.float32)
    return {"ident": ident, "identb": ident.astype(bf16), "kconst": kconst.astype(bf16),
            "qconst": qconst.astype(bf16), "maxsel": maxsel.astype(bf16), "prefmask": prefmask.astype(bf16),
            "prefmaskT": prefmaskT.astype(bf16), "headsel": headsel, "selgrp": selgrp,
            "upper": upper.astype(bf16), "onesb": np.ones((128, 128), bf16), "upto": upto, "steps": steps}


def kernel(**inputs):
    import numpy as np
    import ml_dtypes
    import concourse.bacc as bacc
    from concourse import mybir
    from concourse.bass_utils import run_bass_kernel_spmd

    a = {n: np.asarray(inputs[n]) for n in _WEIGHTS}
    x, wqkv, wo, gw, gb, w1, b1, w2, b2, gamma, beta = (a[n] for n in _WEIGHTS)
    arrays = {
        "x": x.reshape(2048, 128), "wqkvT": np.ascontiguousarray(wqkv.T), "woT": np.ascontiguousarray(wo.T),
        "gateW": gw, "gateb": gb, "W1": w1, "W2": w2,
        "bias": np.concatenate([b1[:, 0:128], b1[:, 128:256], b2]).reshape(128, 24),
        "gamma": gamma, "beta": beta,
    }
    arrays.update(_constants(np, ml_dtypes.bfloat16))
    nc = bacc.Bacc("TRN2", target_bir_lowering=False, num_devices=1)
    args = [nc.dram_tensor("in_" + n, v.shape, mybir.dt.from_np(v.dtype), kind="ExternalInput").ap()
            for n, v in arrays.items()]
    out = nc.dram_tensor("out_0", (2048, 128), mybir.dt.float32, kind="ExternalOutput").ap()
    preln_block_kernel(nc, *args, out)
    r = run_bass_kernel_spmd(nc, [{"in_" + n: np.ascontiguousarray(v) for n, v in arrays.items()}], core_ids=[0])
    return r.results[0]["out_0"].reshape(2, 1024, 128)
```

```python
import concourse.bass as bass
from concourse import mybir
from contextlib import ExitStack


def preln_block_kernel(nc, x, wqkvT, woT, gateW, gateb, W1, W2, bias, gamma, beta,
                       ident, identb, kconst, qconst, maxsel, prefmask, prefmaskT,
                       headsel, selgrp, upper, onesb, upto, steps, out):
    fp32 = mybir.dt.float32
    bf16 = mybir.dt.bfloat16
    i32 = mybir.dt.int32
    ALU = mybir.AluOpType
    ACT = mybir.ActivationFunctionType
    AX = mybir.AxisListType

    D = 128
    NH, HD = 16, 8
    SEQ = 1024
    W, PRE = 64, 16
    ST = 512
    NS = 4
    NT = ST // 128
    NC = ST // W
    NB = NS // 2
    BT = SEQ // 128
    E, HID = 8, 256
    NBLK = BT + E - 1
    CH = 5
    NCH = NBLK // CH
    NPROD = 6
    ROWS = NPROD * HD
    MROW = ROWS + 1
    NU = NT * 5
    EPS = 1e-5
    SCALE = float(HD) ** -0.5
    XM = 64

    QPUT = [(0, 0, 3, 1), (1, 3, 5, 1), (2, 5, 6, 1)]
    KPUT = [(0, 1, 6, 2), (1, 2, 5, 2), (2, 0, 1, 1)]

    qd = nc.dram_tensor("qstack", [NS, NH, HD, NPROD, ST], bf16).ap()
    kd = nc.dram_tensor("kstack", [NB, NH, HD, NPROD, SEQ], bf16).ap()
    xs = [nc.dram_tensor(f"slots_in{b}", [NBLK * 128, D], fp32).ap() for b in range(NB)]
    ys = [nc.dram_tensor(f"slots_out{i}", [NBLK * 128, D], fp32).ap() for i in range(2 * NB)]

    ctx = ExitStack()
    with ctx:
        def sb(name, shape, dt=fp32):
            return ctx.enter_context(nc.sbuf_tensor(name, shape, dt))

        def sem(name):
            return ctx.enter_context(nc.semaphore(name))

        wqkv_s = sb("wqkv_s", [128, 3 * D])
        wo_s = sb("wo_s", [128, D])
        gw_s = sb("gw_s", [128, E])
        gb_s = sb("gb_s", [128, E])
        w1_s = sb("w1_s", [128, 2, E * 128])
        w2_s = sb("w2_s", [128, 2, E * D])
        bias_s = sb("bias_s", [128, 24])
        bpart = sb("bpart", [3, 3, E * 128], bf16)
        bp = sb("bp", [128, 3, 24], bf16)
        br = sb("br", [128, 24])
        gam_s = sb("gam_s", [128, D])
        bet_s = sb("bet_s", [128, D])
        id_s = sb("id_s", [128, 128])
        idb_s = sb("idb_s", [128, 128], bf16)
        up_s = sb("up_s", [128, 128], bf16)
        ones_s = sb("ones_s", [128, 128], bf16)
        upto_s = sb("upto_s", [128, E, E])
        steps_s = sb("steps_s", [128, 16])
        msel_s = sb("msel_s", [NH, 2, 128], bf16)
        pm_s = sb("pm_s", [128, NH * PRE], bf16)
        pmT_s = sb("pmT_s", [128, 128], bf16)
        hsel_s = sb("hsel_s", [128, NH])
        gsel_s = sb("gsel_s", [128, NH])
        half_s = sb("half_s", [128, NT])
        zero_s = sb("zero_s", [128, D])
        x_s = sb("x_s", [128, NS, NT, D])
        st6 = sb("st6", [128, NT, 6])
        mv = sb("mv", [128, NT, 2])
        veps = sb("veps", [128, NT])
        rstd = sb("rstd", [128, NT])
        mv3 = sb("mv3", [128, 2, NT, 2])
        rstd3 = sb("rstd3", [128, 2, NT])
        scr = sb("scr", [128, 2, ST])
        kr = scr[:, 0, :]
        qr = scr[:, 1, :]
        bst = scr[:, :, :].rearrange("p a t -> p (a t)").rearrange("p (t d) -> p t d", d=D)
        xnT = sb("xnT", [128, 2, XM + ST])
        kf = sb("kf", [128, ST])
        qf = sb("qf", [128, 2, ST])
        parts = sb("parts", [128, 2, 3, ST], bf16)
        kp = parts[:, 0]
        qp = parts[:, 1]
        yg = parts[:, :, :, :].rearrange("p a j t -> p (a j t)").bitcast(fp32)\
            .rearrange("p (t d) -> p t d", d=D)[:, 0:BT]
        xg = sb("xg", [128, 8, PRE])
        kg = sb("kg", [128, 2, NH, PRE])
        vg = sb("vg", [128, 2, 4, 4, 32])
        vaug = sb("vaug", [128, 2, 2, NT, NH, HD + 1])
        QS = sb("QS", [128, 2, NH, ST], bf16)
        KS = sb("KS", [128, 2, NH, NC, 2 * W], bf16)
        m4 = sb("m4", [128, NT, NH])
        mg = sb("mg", [128, NT, NH])
        mt = sb("mt", [128, NT, NH])
        mh = sb("mh", [NH, ST], bf16)
        ml = sb("ml", [NH, ST], bf16)
        pgx = sb("pgx", [128, 2 * CH * D])
        PG = pgx[:, 0:2 * ST].rearrange("p (g t) -> p g t", g=2)
        xns = [a.rearrange("p (t d) -> p t d", t=NT) for a in (PG[:, 0, :], PG[:, 1, :], qr, qr)]
        xin = pgx[:, :].rearrange("p (a j d) -> p a j d", a=2, j=CH)
        PT = sb("PT", [128, 2, NH, W])
        ptf = PT[:, :].rearrange("p a h q -> p (a h q)")
        early = ptf.bitcast(bf16)
        kc_s = early[:, 0:4 * ST].rearrange("p (a t) -> p a t", a=2)
        qc_s = early[:, 4 * ST:5 * ST]
        oS = sb("oS", [128, 2, 4, 256])
        rden = sb("rden", [128, 2, NH])
        otok = sb("otok", [128, 2, NH, HD])
        oT = sb("oT", [128, 2, D])
        xn2 = sb("xn2", [128, NS, NT, D])
        xn2T = kf
        lg = sb("lg", [128, NB, BT, E])
        lg2 = sb("lg2", [128, BT, E])
        tmp8 = sb("tmp8", [128, BT, E])
        pk = sb("pk", [128, BT, 2])
        top = sb("top", [128, 2, BT])
        oh = sb("oh", [128, BT, 2, E])
        ohb = sb("ohb", [128, BT, 2, E], bf16)
        dif = sb("dif", [128, BT, E + 1])
        ex = sb("ex", [128, BT, E + 1])
        dn = sb("dn", [128, BT])
        rdn = sb("rdn", [128, BT])
        val = sb("val", [128, NB, BT, 2])
        cnt = sb("cnt", [128, 2 * E])
        big = sb("big", [128, 2 * NBLK * E])
        cmp_ = big[:, 0:2 * E * BT].rearrange("p (c j) -> p c j", j=BT)
        pre = big[:, 0:2 * E * E].rearrange("p (r e f) -> p r e f", r=2, f=E)
        slot_of = big[:, 0:BT * 2 * E].rearrange("p (t c) -> p t c", t=BT)
        over = big[:, :].rearrange("p (r j e) -> p r j e", r=2, e=E)
        nblk = sb("nblk", [128, 2, E])
        endb = sb("endb", [128, 2, E])
        begb = sb("begb", [128, 2 * E])
        posf = sb("posf", [128, BT, 2])
        pos = sb("pos", [128, NB, BT, 2], i32)
        ebf = sb("ebf", [128, 2, NBLK])
        eb = sb("eb", [128, NB, 2, 16], i32)
        xT = oS[:, 0, 0, :].rearrange("p (a m) -> p a m", a=2)
        hs = oS[:, 0, 1:3, :]
        hT = oS[:, 1, 0:2, :]
        yb = ptf[:, 0:2 * CH * D].rearrange("p (a j d) -> p a j d", a=2, j=CH)

        pb = [ctx.enter_context(nc.psum_tensor(f"bank{i}", [128, 512], fp32)) for i in range(2)]
        ring = ctx.enter_context(nc.psum_tensor("ring", [128, 4, 512], fp32))
        pa = [ctx.enter_context(nc.psum_tensor(f"aux{i}", [128, 512], fp32)) for i in range(2)]

        names = """w_in x_in0 x_in1 x_in2 x_in3 c_in i_in f_in bp_ok bp_in st_init vones stats rstd_ok xn_ok
            xnT_ps xnT_ok k_ps q_ps v_ps vg_ps kf_ok qf_ok kh_ok km_ok qh_ok qr_ok qm_ok xb_ok v_ok vg_ok kg_ok xg_ok kparts qparts kd_wr qd_wr
            ks_in00 ks_in01 ks_in02 ks_in03 ks_in10 ks_in11 ks_in12 ks_in13 qs_in0 qs_in1 s1_ps max_ok mt_ok mT_ps mhl m_in pg_ps pg_ok s2_ps pt_ok pv_ok oS_ok oT_ps otok_ok
            o2_ps oT_ok att_ps x1_ok stats2 rstd2_ok xn2_ok xn2T_ps xn2T_ok lg_ps lg_ok oh_ok dif_ok ex_ok
            pos_ps pos_ok eb_ok zs_ok zs_wr xs_wr0 xs_wr1 xs_wr2 xs_wr3 xin_first xin_in0 xin_in1 xT_ps xT_ok hm_ps hs_ok hT_ps hT_ok y_ps yb_ok ys_wr0 ys_wr1
            yga_in ygb_in bst_ok yg_used z_ok stats3 rstd3_ok outs_ok out_wr dchain pchain""".split()
        s = {n: sem(n) for n in names}
        block = ctx.enter_context(nc.Block())

        ORDER = ["L0", "L1", "A0", "A1", "C0", "L2", "D0", "A2", "E0", "L3", "D1", "A3", "E1", "D2", "E2",
                 "D3", "E3", "G1", "R0", "M0", "M1", "N0", "N1"]
        GATHERS = ["M0", "M1", "N0", "N1"]

        def run(**stages):
            for st in ORDER:
                if st[0] in stages:
                    stages[st[0]](int(st[1]))

        def psum_read(eng, st, ring_only=False):
            k, n = st[0], int(st[1])
            if k == "A":
                eng.wait_ge(s["v_ok"], 2 * (n + 1))
                eng.wait_ge(s["vg_ok"], 2 * (n // 2 + 1))
            if ring_only and k == "D":
                eng.wait_ge(s["pt_ok"], NC * (n + 1))
                return
            if k == "C" or (k == "D" and n + 1 < NS):
                eng.wait_ge(s["mhl"], 2 * (n + 1) + (2 if k == "D" else 0))
            if k == "D":
                eng.wait_ge(s["pt_ok"], NC * (n + 1))
                eng.wait_ge(s["oS_ok"], 4 * (n + 1))
            if st == "D3":
                eng.wait_ge(s["pos_ok"], 1)
            if k == "E":
                eng.wait_ge(s["x1_ok"], NT * (n + 1))

        def stage_before(st):
            i = ORDER.index(st) - 1
            while ORDER[i][0] in "LMN":
                i -= 1
            return ORDER[i]

        def stage_after(st):
            return next(q for q in ORDER[ORDER.index(st) + 1:] if q[0] not in "LMN")

        def done(kind, st):
            return sum(q[0] == kind for q in ORDER[:ORDER.index(st)])

        def rows_stored(eng, i):
            end = NCH * (i + 1)
            eng.wait_ge(s["ys_wr0"], 32 * ((end + 1) // 2))
            eng.wait_ge(s["ys_wr1"], 32 * (end // 2))

        def aux_bank(n, u):
            return [pa[0], pa[1], ring[:, 0], ring[:, 1], ring[:, 2], ring[:, 3]][u % 6] if n == 0 else pa[u % 2]

        def y_bank(i):
            return pb[0] if i < SHARE else pb[i % 2]

        def gate_bank(n):
            return pa[1] if n < NS - 1 else pb[1]

        def count_bank(b):
            bank = pa[0] if b == 0 else pb[1]
            return bank[:, 0:BT * 2 * E], bank[:, BT * 2 * E:(BT + 1) * 2 * E]

        def units_at(n, c):
            first = 0 if n == 0 else 1
            return range(NU * max(c - first, 0) // (NC - first), NU * max(c + 1 - first, 0) // (NC - first))

        ALL = NBLK * 2 * NB
        GATE_STEP, EX_STEP, COUNT_STEP = 2, 7, 6
        LENT = 10
        SHARE = 7

        def token_copy(eng, copy, i):
            eng.wait_ge(s["xT_ps"], i + 1)
            if i >= 2:
                eng.wait_ge(s["hm_ps"], i - 1)
            copy(xT[:, i % 2, :], pa[i % 2][:, 0:128]).then_inc(s["xT_ok"], 1)

        def hidden_copy(eng, copy, i):
            eng.wait_ge(s["hT_ps"], i + 1)
            if i >= 2:
                eng.wait_ge(s["y_ps"], i - 1)
            copy(hT[:, i % 2, :], ring[:, 2 + i % 2, 0:HID]).then_inc(s["hT_ok"], 1)

        xv = x.rearrange("(s t p) d -> s p t d", t=NT, p=128)
        ov = out.rearrange("(s t p) d -> s p t d", t=NT, p=128)

        @block.sync
        def _(sp):
            sp.dma_start(x_s[:, 0], xv[0]).then_inc(s["x_in0"], 16)
            sp.dma_start(id_s[:, :], ident).then_inc(s["i_in"], 16)
            for dst, src in ((wqkv_s[:, :], wqkvT), (hsel_s[:, :], headsel), (gsel_s[:, :], selgrp),
                             (wo_s[:, :], woT), (bias_s[:, :], bias)):
                sp.dma_start(dst, src).then_inc(s["w_in"], 16)
            for n in range(1, NS):
                sp.dma_start(x_s[:, n], xv[n]).then_inc(s[f"x_in{n}"], 16)

            def stacks(n):
                slot, b, c0 = n % 2, n // 2, (n % 2) * ST
                for p, j0, j1, dj in KPUT:
                    sp.wait_ge(s[("kh_ok", "km_ok", "kparts")[p]], n + 1)
                    nj = len(range(j0, j1, dj))
                    sp.dma_start(kd[b].rearrange("h d j t -> (h d) j t")[:, j0:j1:dj, c0:c0 + ST],
                                 kp[:, p, None, :].broadcast_to((128, nj, ST))).then_inc(s["kd_wr"], 16)
                for p, j0, j1, dj in QPUT:
                    sp.wait_ge(s[("qh_ok", "qm_ok", "qparts")[p]], n + 1)
                    nj = len(range(j0, j1, dj))
                    sp.dma_start(qd[n].rearrange("h d j t -> (h d) j t")[:, j0:j1:dj, :],
                                 qp[:, p, None, :].broadcast_to((128, nj, ST))).then_inc(s["qd_wr"], 16)
                if n >= 2:
                    sp.wait_ge(s["s2_ps"], NC * (n - 1))
                sp.wait_ge(s["kd_wr"], 48 * (n + 1))
                if n < 2:
                    sp.wait_ge(s["st_init"], 3 * n + 1)
                kv = kd[b].rearrange("h d j t -> (d j) h t")
                for c in range(NC):
                    if c == 2:
                        sp.wait_ge(s["qd_wr"], 48 * (n + 1))
                        if n < 2:
                            sp.wait_ge(s["st_init"], 3 * n + 2)
                        sp.dma_start(QS[0:ROWS, slot, :, :], qd[n].rearrange("h d j t -> (d j) h t"))\
                            .then_inc(s[f"qs_in{slot}"], 16)
                        sp.dma_start(QS[MROW:MROW + 2, slot, :, :],
                                     qconst[MROW:MROW + 2, None, :].broadcast_to((2, NH, ST))).then_inc(s[f"qs_in{slot}"], 16)
                    if c == NC // 2 and n < 2:
                        sp.wait_ge(s["st_init"], 3 * n + 3)
                    if c0 + c == 0:
                        src, dst = kv[:, :, 0:W], KS[0:ROWS, slot, :, c, W:2 * W]
                    else:
                        src, dst = kv[:, :, c0 + (c - 1) * W:c0 + (c + 1) * W], KS[0:ROWS, slot, :, c, :]
                    sp.dma_start(dst, src).then_inc(s[f"ks_in{slot}{c // 2}"], 16)


            def maxima(n):
                sp.wait_ge(s["mhl"], 2 * (n + 1))
                sp.dma_start(QS[MROW:MROW + 1, n % 2, :, :], mh[:, :]).then_inc(s["m_in"], 16)
                sp.dma_start(QS[MROW + 1:MROW + 2, n % 2, :, :], ml[:, :]).then_inc(s["m_in"], 16)

            fs = [(gw_s[:, :], gateW), (gb_s[:, :], gateb[None, :].broadcast_to((128, E))),
                  (up_s[:, :], upper), (ones_s[:, :], onesb), (upto_s[:, :, :], upto), (steps_s[:, :], steps),
                  (gam_s[:, :], gamma[None, :].broadcast_to((128, D))),
                  (bet_s[:, :], beta[None, :].broadcast_to((128, D)))]
            for a in range(2):
                fs.append((w1_s[:, a, :].rearrange("p (e c) -> p e c", e=E),
                           W1[:, :, a * 128:(a + 1) * 128].rearrange("e d c -> d e c")))
                fs.append((w2_s[:, a, :].rearrange("p (e c) -> p e c", e=E),
                           W2[:, a * 128:(a + 1) * 128, :].rearrange("e p d -> p e d")))

            def slots_and_biases():
                sp.wait_ge(s["bp_ok"], 1)
                for p in range(3):
                    sp.dma_start(bpart[p:p + 1, :, :].rearrange("o a c -> o (a c)"), bp[:, p, :])\
                        .then_inc(s["bp_in"], 16)
                sp.wait_ge(s["zs_ok"], 1)
                for b in range(NB):
                    sp.dma_start(xs[b].rearrange("(j p) d -> p j d", p=128),
                                 zero_s[:, None, :].broadcast_to((128, NBLK, D))).then_inc(s["zs_wr"], 16)

            def late_loads():
                for dst, src in fs:
                    sp.dma_start(dst, src).then_inc(s["f_in"], 16)

            def D_(n):
                if n == 0:
                    sp.wait_ge(s["m_in"], 32)
                    late_loads()
                    slots_and_biases()
                if n + 1 < NS:
                    maxima(n + 1)

            def R_(_):
                for K in range(NCH * 2 * NB):
                    i, k = K // NCH, K % NCH
                    sp.wait_ge(s[f"xs_wr{i}"], 16 * BT)
                    if K < 2:
                        sp.wait_ge(s["pv_ok"], NC * NS)
                    else:
                        sp.wait_ge(s["xT_ps"], CH * (K - 1))
                    rows = xs[i % NB].rearrange("(k j p) d -> k p j d", j=CH, p=128)[k]
                    if k == 0:
                        sp.dma_start(xin[:, K % 2, 0:1], rows[:, 0:1]).then_inc(s["xin_first"], 16)
                        sp.dma_start(xin[:, K % 2, 1:CH], rows[:, 1:CH]).then_inc(s[f"xin_in{K % 2}"], 16)
                    else:
                        sp.dma_start(xin[:, K % 2], rows).then_inc(s[f"xin_in{K % 2}"], 16)

            def N_(b):
                for n in (2 * b, 2 * b + 1):
                    sp.wait_ge(s["outs_ok"], n + 1)
                    sp.dma_start(ov[n], xn2[:, n]).then_inc(s["out_wr"], 16)

            run(A=stacks, C=maxima, D=D_, R=R_, N=N_)
            sp.wait_ge(s["out_wr"], 16 * NS)

        @block.gpsimd
        def _(pool):
            count = [0]

            def link(ins):
                count[0] += 1
                ins.then_inc(s["pchain"], 1)
                pool.wait_ge(s["pchain"], count[0])

            nc.gpsimd.memset(half_s[:, :], -0.5).then_inc(s["vones"], 1)
            nc.gpsimd.memset(xnT[:, 0, 0:XM], 0.0).then_inc(s["vones"], 1)
            nc.gpsimd.memset(zero_s[:, :], 0.0).then_inc(s["zs_ok"], 1)
            pool.wait_ge(s["vones"], 2)

            def inv_std(var_ok, n, done, count=None, mv=mv, rstd=rstd):
                pool.wait_ge(s[var_ok], count or n + 1)
                link(nc.gpsimd.tensor_scalar(veps[:, :], mv[:, :, 1], EPS, None, ALU.add))
                nc.gpsimd.tensor_tensor(rstd[:, :], veps[:, :], half_s[:, :], ALU.pow).then_inc(s[done], 1)

            def L_(n):
                inv_std("stats", n, "rstd_ok")
                if n == 0:
                    nc.gpsimd.memset(vg[:], 0.0).then_inc(s["vones"], 1)
                    nc.gpsimd.memset(vaug[:], 1.0).then_inc(s["vones"], 1)

            def A_(n):
                pool.wait_ge(s["qh_ok"], n + 1)
                q = qf[:, n % 2, :]
                nc.gpsimd.tensor_tensor(qr, q, qp[:, 0, :], ALU.subtract).then_inc(s["qr_ok"], 1)
                pool.wait_ge(s["qm_ok"], n + 1)
                nc.gpsimd.tensor_tensor(qp[:, 2, :], qr, qp[:, 1, :], ALU.subtract)\
                    .then_inc(s["qparts"], 1)

            def E_(n):
                inv_std("stats2", n, "rstd2_ok")
                if n == 0:
                    pool.wait_ge(s["f_in"], 12 * 16)
                pool.wait_ge(s["xn2_ok"], NT * (n + 1))
                nc.gpsimd.tensor_tensor(x_s[:, n], x_s[:, n], bet_s[:, None, :].broadcast_to((128, NT, D)), ALU.add)\
                    .then_inc(s["xb_ok"], 1)

            def scatter(b, r, t, rows):
                nc.gpsimd.indirect_dma_start(
                    out=xs[b], out_offset=bass.IndirectOffsetOnAxis(ap=pos[:, b, t, r:r + 1], axis=0),
                    in_=rows, in_offset=None).then_inc(s[f"xs_wr{NB * r + b}"], 16)

            def G_(b):
                pool.wait_ge(s["pos_ok"], b + 1)
                pool.wait_ge(s["zs_wr"], 16 * NB)
                for t in range(BT):
                    scatter(b, 0, t, xn2[:, 2 * b + t // NT, t % NT, :])

            def gathers(st, b, r):
                q = GATHERS.index(st)
                rows_stored(pool, NB * r + b)
                if q == 0:
                    pool.wait_ge(s["kd_wr"], 48 * NS)
                    pool.wait_ge(s["qd_wr"], 48 * NS)
                for t in range(BT):
                    if q >= 1 and t % NT == 0:
                        pool.wait_ge(s["yg_used"], 4 * (q - 1) + 2 * (t // NT) + 2)
                    nc.gpsimd.indirect_dma_start(
                        out=yg[:, t, :], out_offset=None, in_=ys[NB * r + b],
                        in_offset=bass.IndirectOffsetOnAxis(ap=pos[:, b, t, r:r + 1], axis=0))\
                        .then_inc(s["yga_in" if t < NT else "ygb_in"], 16)

            def M_(b):
                gathers(f"M{b}", b, 0)
                for t in range(BT):
                    if t % NT == 0:
                        pool.wait_ge(s["bst_ok"], 2 * b + t // NT + 1)
                    scatter(b, 1, t, bst[:, t, :])

            def N_(b):
                gathers(f"N{b}", b, 1)
                for n in (2 * b, 2 * b + 1):
                    inv_std("stats3", n, "rstd3_ok", 2 * (n + 1), mv3[:, n % 2], rstd3[:, n % 2])
                    if b == 0:
                        finish(n)

            def finish(n):
                z = xn2[:, n]
                pool.wait_ge(s["rstd3_ok"], n + 1)
                pool.wait_ge(s["z_ok"], n + 1)
                link(nc.gpsimd.tensor_tensor(z, z, rstd3[:, n, :, None].broadcast_to((128, NT, D)), ALU.mult))
                nc.gpsimd.tensor_tensor(z, z, x_s[:, n], ALU.add).then_inc(s["outs_ok"], 1)

            def D_(n):
                if n == NS - 1:
                    G_(0)

            run(L=L_, A=A_, D=D_, E=E_, G=G_, M=M_, N=N_)

        @block.scalar
        def _(act):
            cs = [(kc_s[:, :, :], kconst), (qc_s[:, :], qconst), (idb_s[:, :], identb),
                  (pm_s[:, :], prefmask), (pmT_s[:, :], prefmaskT), (msel_s[:, :, :], maxsel)]
            for dst, src in cs:
                act.dma_start(dst, src).then_inc(s["c_in"], 16)
            def turned_tokens(n):
                slot = n % 2
                act.wait_ge(s["xnT_ps"], n + 1)
                if n == 0:
                    act.wait_ge(s["vones"], 2)
                if n >= 2:
                    act.wait_ge(s["v_ps"], 2 * (n - 1))
                if slot == 0:
                    if n >= 2:
                        act.wait_ge(s["v_ps"], 2 * n)
                        act.wait_ge(s["xg_ok"], n // 2)
                    nc.scalar.copy(xnT[:, 1, 0:XM], pa[1][:, ST - XM:ST]).then_inc(s["xnT_ok"], 1)
                nc.scalar.copy(xnT[:, slot, XM:XM + ST], pa[1][:, :]).then_inc(s["xnT_ok"], 1)

            def A_(n):
                slot = n % 2
                if n < 2:
                    turned_tokens(n)
                act.wait_ge(s["k_ps"], n + 1)
                if n >= 1:
                    act.wait_ge(s["kparts"], n)
                if done("E", f"A{n}"):
                    act.wait_ge(s["lg_ps"], done("E", f"A{n}"))
                nc.scalar.copy(kf[:, :], ring[:, 0, :]).then_inc(s["kf_ok"], 1)
                if n >= 1:
                    act.wait_ge(s["kd_wr"], 48 * n)
                nc.scalar.copy(kp[:, 0, :], ring[:, 0, :]).then_inc(s["kh_ok"], 1)
                act.wait_ge(s["q_ps"], n + 1)
                if n >= 2:
                    act.wait_ge(s["pg_ps"], 2 * (n - 1))
                    act.wait_ge(s["qparts"], n - 1)
                nc.scalar.mul(qf[:, slot, :], ring[:, 1, :], SCALE).then_inc(s["qf_ok"], 1)
                if n >= 1:
                    act.wait_ge(s["qd_wr"], 48 * n)
                nc.scalar.mul(qp[:, 0, :], ring[:, 1, :], SCALE).then_inc(s["qh_ok"], 1)
                if n == 0:
                    act.wait_ge(s["vones"], 4)
                if n >= 2:
                    act.wait_ge(s["pv_ok"], NC * (n - 1))
                for k in range(2):
                    act.wait_ge(s["v_ps"], 2 * n + k + 1)
                    nc.scalar.copy(vaug[:, slot, k, :, :, 0:HD],
                                   ring[:, 2 + k, :].rearrange("p (t h d) -> p t h d", t=NT, d=HD))\
                        .then_inc(s["v_ok"], 1)
                act.wait_ge(s["qr_ok"], n + 1)
                nc.scalar.copy(qp[:, 1, :], qr).then_inc(s["qm_ok"], 1)

            def D_(n):
                for k, g in enumerate((1, 0)):
                    act.wait_ge(s["pg_ps"], 2 * n + k + 1)
                    if n >= 1 and k == 0:
                        act.wait_ge(s["pv_ok"], NC * n)
                    nc.scalar.activation(PG[:, g, :], pa[g][:, :], ACT.Exp).then_inc(s["pg_ok"], 1)
                for c in range(NC):
                    i = NC * n + c
                    act.wait_ge(s["s2_ps"], i + 1)
                    if i >= 2:
                        act.wait_ge(s["pv_ok"], i - 1)
                    nc.scalar.activation(PT[:, i % 2].rearrange("p (g h) q -> p g (h q)", g=2),
                                         ring[:, 2 * (i % 2):2 * (i % 2) + 2, :], ACT.Exp)\
                        .then_inc(s["pt_ok"], 1)
                    if c == 1 and n >= 1:
                        gate_operand(n - 1)
                    if c % 4 == 0 and c > 0:
                        output(n, c // 4 - 1)
                    if n == NS - 1 and c == 1:
                        G_(0)
                if n + 2 < NS:
                    turned_tokens(n + 2)
                output(n, 1)

            def output(n, hf):
                act.wait_ge(s["pv_ok"], NC * n + 4 * (hf + 1))
                if n >= 1 and hf == 0:
                    act.wait_ge(s["oT_ps"], NT * n)
                nc.scalar.copy(oS[:, hf, 0:2], pb[0][:, :].rearrange("p (g q) -> p g q", g=2))\
                    .then_inc(s["oS_ok"], 1)

            def E_(n):
                for t in range(NT):
                    i = NT * n + t
                    act.wait_ge(s["o2_ps"], i + 1)
                    if i >= 2:
                        act.wait_ge(s["att_ps"], i - 1)
                    nc.scalar.copy(oT[:, i % 2, :], ring[:, t, 0:D]).then_inc(s["oT_ok"], 1)

            def gate_operand(n):
                act.wait_ge(s["xn2T_ps"], n + 1)
                if n >= 1:
                    act.wait_ge(s["lg_ps"], n)
                act.wait_ge(s["kparts"], min(n + 3, NS))
                nc.scalar.copy(xn2T[:, :], gate_bank(n)[:, :]).then_inc(s["xn2T_ok"], 1)

            def G_(b):
                act.wait_ge(s["dif_ok"], b + 1)
                nc.scalar.activation(ex[:, :, :], dif[:, :, :], ACT.Exp).then_inc(s["ex_ok"], 1)

            def R_(_):
                for st in range(ALL + 3):
                    if st == GATE_STEP + 1:
                        gate_operand(3)
                    if st == EX_STEP:
                        G_(1)
                    i = st - 3
                    if i >= 0:
                        K = i // CH
                        act.wait_ge(s["y_ps"], i + 1)
                        if K >= 2 and i % CH == 0:
                            act.wait_ge(s[f"ys_wr{K % 2}"], 32 * (K // 2))
                        nc.scalar.copy(yb[:, K % 2, i % CH, :], y_bank(i)[:, 0:D]).then_inc(s["yb_ok"], 1)
                        if i % CH >= CH - 2:
                            j = slice(0, CH - 1) if i % CH == CH - 2 else slice(CH - 1, CH)
                            act.wait_ge(s["yb_ok"], i + 1)
                            act.dma_start(ys[K // NCH].rearrange("(k j p) d -> k p j d", j=CH, p=128)[K % NCH, :, j],
                                          yb[:, K % 2, j]).then_inc(s[f"ys_wr{K % 2}"], 16)
                    i = st - 2
                    if 0 <= i < LENT:
                        hidden_copy(act, nc.scalar.copy, i)
                    i = st - 1
                    if 0 <= i < ALL:
                        act.wait_ge(s["hm_ps"], i + 1)
                        if i >= 2:
                            act.wait_ge(s["hT_ps"], i - 1)
                        nc.scalar.activation(hs[:, i % 2, :], ring[:, i % 2, 0:HID], ACT.Relu)\
                            .then_inc(s["hs_ok"], 1)
                    if st < LENT:
                        token_copy(act, nc.scalar.copy, st)

            run(A=A_, D=D_, E=E_, R=R_)

        @block.tensor
        def _(pe):
            mm = nc.tensor.matmul

            def turn_tokens(n):
                pe.wait_ge(s["xn_ok"], NT * (n + 1))
                for t in range(NT):
                    last = nc.tensor.transpose(pa[1][:, t * 128:(t + 1) * 128], xns[n][:, t, :], id_s[:, :])
                last.then_inc(s["xnT_ps"], 1)

            def A_(n):
                slot = n % 2
                if n == 0:
                    pe.wait_ge(s["i_in"], 16)
                if n == 1:
                    pe.wait_ge(s["xnT_ok"], 2)
                if n < 2:
                    turn_tokens(n)
                if n >= 1:
                    psum_read(pe, stage_before(f"A{n}"), ring_only=True)
                pe.wait_ge(s["xnT_ok"], n + 1 + n // 2 + 1)
                if n == 0:
                    pe.wait_ge(s["w_in"], 5 * 16)
                xt = xnT[:, slot, XM:XM + ST]
                mm(ring[:, 0, :], wqkv_s[:, D:2 * D], xt, start=True, stop=True).then_inc(s["k_ps"], 1)
                mm(ring[:, 1, :], wqkv_s[:, 0:D], xt, start=True, stop=True).then_inc(s["q_ps"], 1)
                for k in range(2):
                    for t in range(NT):
                        c = t * 128 + (XM if k == 0 else 0)
                        last = mm(ring[:, 2 + k, t * 128:(t + 1) * 128], xnT[:, slot, c:c + 128],
                                  wqkv_s[:, 2 * D:3 * D], start=True, stop=True)
                    last.then_inc(s["v_ps"], 1)
                if slot == 0:
                    pe.wait_ge(s["xg_ok"], n // 2 + 1)
                    pe.wait_ge(s["kh_ok"], n + 1)
                    mm(ring[:, 0, 0:D], xg[:, :, :].rearrange("p a k -> p (a k)"), wqkv_s[:, 2 * D:3 * D],
                       start=True, stop=True).then_inc(s["vg_ps"], 1)

            def unit(n, u):
                slot, b, t, g = n % 2, n // 2, u // 5, u % 5
                i = NU * n + u
                banks = 6 if n == 0 else 2
                if u >= banks or n >= 1:
                    pe.wait_ge(s["max_ok"], i + 1 - banks)
                dst = aux_bank(n, u)
                if g == 0:
                    pe.wait_ge(s[f"ks_in{slot}{t}"], 32 * (b + 1))
                if g < 4:
                    for hh in range(4):
                        for p in range(2):
                            c, h = 2 * t + p, 4 * g + hh
                            last = mm(dst[W * p:W * (p + 1), hh * 128:(hh + 1) * 128],
                                      QS[:, slot, h, c * W:(c + 1) * W], KS[:, slot, h, c, :],
                                      start=(hh == 0), stop=True, skip_group_check=True)
                else:
                    first = slot == 0 and t == 0
                    last = mm(dst[:, 0:NH * PRE], qf[:, slot, t * 128:(t + 1) * 128],
                              kg[:, b].rearrange("p h k -> p (h k)"), start=True, stop=not first)
                    if first:
                        last = mm(dst[:, 0:NH * PRE], idb_s[:, :], pm_s[:, :], start=False, stop=True)
                last.then_inc(s["s1_ps"], 1)

            def operands(n):
                if n == 0:
                    pe.wait_ge(s["c_in"], 96)
                pe.wait_ge(s[f"qs_in{n % 2}"], 32 * (n // 2 + 1))
                pe.wait_ge(s["kg_ok"], n // 2 + 1)

            def turn_maxima(n):
                pe.wait_ge(s["mt_ok"], n + 1)
                for t in range(NT):
                    last = nc.tensor.transpose(pa[0][0:NH, t * 128:(t + 1) * 128], mt[:, t, :], id_s[:, :])
                last.then_inc(s["mT_ps"], 1)

            def C_(n):
                psum_read(pe, stage_before(f"C{n}"))
                operands(n)
                for u in range(NU):
                    unit(n, u)
                turn_maxima(n)

            def prefix_scores(n, g):
                slot, b = n % 2, n // 2
                pe.wait_ge(s["mhl"], 2 * (n + 1))
                mm(pa[g][:, :], kg[:, b, 8 * g:8 * g + 8].rearrange("p h k -> p (h k)"), qf[:, slot, :],
                   start=True, stop=False)
                mm(pa[g][:, :], msel_s[:, g, :], mh[:, :], start=False, stop=False)
                if slot == 0:
                    mm(pa[g][:, 0:PRE], pmT_s[:, :], idb_s[:, 0:PRE], start=False, stop=False)
                mm(pa[g][:, :], msel_s[:, g, :], ml[:, :], start=False, stop=True).then_inc(s["pg_ps"], 1)

            def D_(n):
                slot, b = n % 2, n // 2
                psum_read(pe, stage_before(f"D{n}"))
                if n == 0:
                    for g in (1, 0):
                        prefix_scores(n, g)
                pe.wait_ge(s["v_ok"], 2 * (n + 1))
                pe.wait_ge(s["vg_ok"], 2 * (b + 1))
                pe.wait_ge(s["m_in"], 32 * (n + 1))

                def scores(c):
                    i = NC * n + c
                    if i >= 2:
                        pe.wait_ge(s["pt_ok"], i - 1)
                    for h in range(NH):
                        last = mm(ring[:, 2 * (i % 2) + h // 8, (h % 8) * W:(h % 8 + 1) * W],
                                  KS[:, slot, h, c, :], QS[:, slot, h, c * W:(c + 1) * W],
                                  start=(h % 8 == 0), stop=True, skip_group_check=True)
                    last.then_inc(s["s2_ps"], 1)

                def values(c):
                    i = NC * n + c
                    pe.wait_ge(s["pt_ok"], i + 1)
                    if c % 4 == 0:
                        if i >= 4:
                            pe.wait_ge(s["oS_ok"], i // 2)
                        for g in range(4):
                            mm(pb[g // 2][:, (g % 2) * 256:(g % 2 + 1) * 256],
                               vg[:, b, g].rearrange("p i e -> p (i e)"),
                               PG[:, g // 2, (c // 4) * 256:(c // 4 + 1) * 256],
                               start=(g % 2 == 0), stop=True, skip_group_check=True)
                    for h in range(NH):
                        g, q = h // 4, h % 4
                        col = (g % 2) * 256 + (c % 4) * W
                        last = mm(pb[g // 2][32 * q:32 * q + HD + 1, col:col + W],
                                  vaug[:, slot, 0 if c % 2 else 1, c // 2, h, :], PT[:, i % 2, h, :],
                                  start=False, stop=True, skip_group_check=True)
                    last.then_inc(s["pv_ok"], 1)

                scores(0)
                pe.wait_ge(s["pg_ok"], 2 * (n + 1))
                for c in range(NC):
                    if c + 1 < NC:
                        scores(c + 1)
                    if n >= 1 and c == 1:
                        gate_logits(n - 1)
                        values(c)
                        pe.wait_ge(s["lg_ok"], n)
                    if n + 1 < NS:
                        if c == (0 if n == 0 else 1):
                            operands(n + 1)
                        todo = list(units_at(n, c))
                        for u in todo[:2]:
                            unit(n + 1, u)
                    if n == 0 or c != 1:
                        values(c)
                    if n + 1 < NS:
                        for u in todo[2:]:
                            unit(n + 1, u)
                    if n >= 1 and c == 0:
                        turn_gate_operand(n - 1)
                    if n == NS - 1 and c == 1:
                        G_(0)
                if n + 2 < NS:
                    pe.wait_ge(s["max_ok"], NU * (n + 2))
                    turn_tokens(n + 2)
                if n + 1 < NS and stage_after(f"D{n}")[0] == "A":
                    turn_maxima(n + 1)

            def E_(n):
                after = stage_before(f"E{n}")
                if after[0] == "A":
                    m = int(after[1])
                    pe.wait_ge(s["xnT_ok"], m + 1 + m // 2 + 1)
                for t in range(NT):
                    i = NT * n + t
                    if t >= 2:
                        pe.wait_ge(s["otok_ok"], i - 1)
                    if t == 0 and after[0] != "A" and n + 1 < NS:
                        pe.wait_ge(s["max_ok"], NU * (n + 2))
                    if t % 2 == 0:
                        pe.wait_ge(s["oS_ok"], 4 * n + t + 2)
                    if t == 1:
                        if n + 1 < NS:
                            pe.wait_ge(s["mhl"], 2 * (n + 2))
                        else:
                            pe.wait_ge(s["pos_ok"], 1)
                    for g in range(4):
                        last = nc.tensor.transpose(pa[1 - t % 2][:, g * 128:(g + 1) * 128],
                                                   oS[:, t // 2, g, (t % 2) * 128:(t % 2 + 1) * 128], id_s[:, :])
                    last.then_inc(s["oT_ps"], 1)
                    if t == 0 and after[0] != "A" and n + 1 < NS:
                        turn_maxima(n + 1)
                    if t == 1:
                        psum_read(pe, after if after[0] == "A" else f"D{n}", ring_only=True)
                    if t >= 1:
                        back(i - 1)
                    if t >= 2:
                        project(i - 2)
                back(NT * n + 3)
                if n + 1 < NS:
                    prefix_scores(n + 1, 1)
                project(NT * n + 2)
                project(NT * n + 3)
                if n + 1 < NS:
                    prefix_scores(n + 1, 0)

            def turn_gate_operand(n):
                for t in range(NT):
                    pe.wait_ge(s["xn2_ok"], NT * n + t + 1)
                    last = nc.tensor.transpose(gate_bank(n)[:, t * 128:(t + 1) * 128], xn2[:, n, t, :], id_s[:, :])
                last.then_inc(s["xn2T_ps"], 1)

            def gate_logits(n):
                pe.wait_ge(s["xn2T_ok"], n + 1)
                if n == 0:
                    pe.wait_ge(s["f_in"], 12 * 16)
                for t in range(NT):
                    last = mm(gate_bank(n)[:, t * E:(t + 1) * E], xn2T[:, t * 128:(t + 1) * 128], gw_s[:, :],
                              start=True, stop=True)
                last.then_inc(s["lg_ps"], 1)

            def back(i):
                pe.wait_ge(s["otok_ok"], i + 1)
                nc.tensor.transpose(ring[:, i % 4, 0:D], otok[:, i % 2].rearrange("p h d -> p (h d)"), id_s[:, :])\
                    .then_inc(s["o2_ps"], 1)

            def project(i):
                pe.wait_ge(s["oT_ok"], i + 1)
                mm(ring[:, i % 4, D:2 * D], oT[:, i % 2, :], wo_s[:, :], start=True, stop=True)\
                    .then_inc(s["att_ps"], 1)

            def G_(b):
                pe.wait_ge(s["oh_ok"], b + 1)
                def row(t):
                    return ohb[:, t].rearrange("p r e -> p (r e)")

                C = 2 * E
                before, total = count_bank(b)
                mm(before, up_s[:, :], ohb[:, :, :, :].rearrange("p t r e -> p (t r e)"),
                   start=True, stop=True, skip_group_check=True)
                for t in range(BT - 1):
                    mm(before[:, (t + 1) * C:BT * C].rearrange("p (t c) -> p t c", c=C), ones_s[:, :],
                       row(t)[:, None, :].broadcast_to((128, BT - 1 - t, C)),
                       start=False, stop=True, skip_group_check=True)
                for t in range(BT):
                    last = mm(total, ones_s[:, :], row(t), start=False, stop=True, skip_group_check=True)
                last.then_inc(s["pos_ps"], 1)

            def experts_of(n):
                pe.wait_ge(s["eb_ok"], n % NB + 1)
                return nc.values_load_multi_w_load_instructions(
                    eb[0:1, n % NB, n // NB, 0:NBLK], engines=[mybir.EngineType.PE], min_val=0,
                    max_val=(E - 1) * 128,
                    skip_runtime_bounds_check_because="the kernel clips the expert to the last one")[1]

            def R_(_):
                pe.wait_ge(s["bp_in"], 48)
                off = dict(enumerate(experts_of(0)))
                for st in range(ALL + 3):
                    if st % NBLK == 0 and 0 < st < ALL:
                        off.update({st + k: o for k, o in enumerate(experts_of(st // NBLK))})
                    if 0 <= st - 3:
                        i, o = st - 3, off[st - 3]
                        pe.wait_ge(s["hT_ok"], i + 1)
                        if i >= 1:
                            pe.wait_ge(s["yb_ok"], i if i < SHARE else i - 1)
                        if i == SHARE:
                            pe.wait_ge(s["pos_ok"], 2)
                        for a in range(2):
                            mm(y_bank(i)[:, 0:D], hT[:, i % 2, a * 128:(a + 1) * 128],
                               w2_s[:, a, bass.ds(o, 128)], start=(a == 0), stop=False)
                        mm(y_bank(i)[:, 0:D], ones_s[0:3, :], bpart[0:3, 2, bass.ds(o, 128)],
                           start=False, stop=True).then_inc(s["y_ps"], 1)
                    if 0 <= st - 2 < ALL:
                        i = st - 2
                        pe.wait_ge(s["hs_ok"], i + 1)
                        if i >= 2:
                            pe.wait_ge(s["hT_ok"], i - 1)
                        for a in range(2):
                            last = nc.tensor.transpose(ring[:, 2 + i % 2, a * 128:(a + 1) * 128],
                                                       hs[:, i % 2, a * 128:(a + 1) * 128], id_s[:, :])
                        last.then_inc(s["hT_ps"], 1)
                    if st == 1:
                        psum_read(pe, "E3")
                    if 0 <= st - 1 < ALL:
                        i, o = st - 1, off[st - 1]
                        pe.wait_ge(s["xT_ok"], i + 1)
                        if i >= 2:
                            pe.wait_ge(s["hs_ok"], i - 1)
                        dst = ring[:, i % 2, 0:HID].rearrange("p (a c) -> p a c", a=2)
                        mm(dst, xT[:, i % 2, :], w1_s[:, :, bass.ds(o, 128)], start=True, stop=False)
                        mm(dst, ones_s[0:3, :], bpart[0:3, 0:2, bass.ds(o, 128)], start=False, stop=True)\
                            .then_inc(s["hm_ps"], 1)
                    if st < ALL:
                        i, K = st, st // CH
                        if st % NBLK == 0:
                            pe.wait_ge(s["xin_first"], 16 * (st // NBLK + 1))
                        elif st % CH == 0 or st % NBLK == 1:
                            pe.wait_ge(s[f"xin_in{K % 2}"], 16 * (K // 2 + 1))
                        if i >= 2:
                            pe.wait_ge(s["xT_ok"], i - 1)
                        nc.tensor.transpose(pa[i % 2][:, 0:128], xin[:, K % 2, st % CH, :], id_s[:, :])\
                            .then_inc(s["xT_ps"], 1)
                    if st == GATE_STEP:
                        turn_gate_operand(3)
                    if st == GATE_STEP + 1:
                        gate_logits(3)
                    if st == COUNT_STEP:
                        G_(1)

            run(A=A_, C=C_, D=D_, E=E_, R=R_)

        @block.vector
        def _(dve):
            v = nc.vector
            count = [0]

            def link(ins):
                count[0] += 1
                ins.then_inc(s["dchain"], 1)
                dve.wait_ge(s["dchain"], count[0])

            normed = []

            def stats(src, n, var_ok):
                for name, value in normed:
                    dve.wait_ge(s[name], value)
                for t in range(NT):
                    last = v.bn_stats(st6[:, t, :], src(t))
                link(last)
                for t in range(NT):
                    last = v.bn_aggr(mv[:, t, :], st6[:, t, :])
                last.then_inc(s[var_ok], 1)

            def L_(n):
                if n >= 2:
                    dve.wait_ge(s["xnT_ps"], n)
                    dve.wait_ge(s["qparts"], n)
                dve.wait_ge(s[f"x_in{n}"], 16)
                stats(lambda t: x_s[:, n, t, :], n, "stats")
                dve.wait_ge(s["rstd_ok"], n + 1)
                dve.wait_ge(s["stats"], n + 1)
                for t in range(NT):
                    v.tensor_scalar(xns[n][:, t, :], x_s[:, n, t, :], mv[:, t, 0:1], rstd[:, t:t + 1],
                                    ALU.subtract, ALU.mult).then_inc(s["xn_ok"], 1)
                normed[:] = [("xn_ok", NT * (n + 1))]
                if n == 0:
                    constant_rows(n, 0)
                if n == 2:
                    link(v.tensor_copy(bp[:, 0, :], bias_s[:, :]))
                    link(v.tensor_tensor(br[:, :], bias_s[:, :], bp[:, 0, :], ALU.subtract))
                    link(v.tensor_copy(bp[:, 1, :], br[:, :]))
                    v.tensor_tensor(bp[:, 2, :], br[:, :], bp[:, 1, :], ALU.subtract).then_inc(s["bp_ok"], 1)

            def constant_rows(n, part):
                dve.wait_ge(s["c_in"], 96)
                if part == 1:
                    ins = v.tensor_copy(QS[:, n, :, :], qc_s[:, None, :].broadcast_to((128, NH, ST)))
                else:
                    half = slice(part // 2 * NC // 2, (part // 2 + 1) * NC // 2)
                    rows = kc_s[:, n].rearrange("p (c k) -> p c k", c=NC)[:, half]
                    ins = v.tensor_copy(KS[:, n, :, half, :].rearrange("p h c k -> p h (c k)"),
                                        rows.rearrange("p c k -> p (c k)")[:, None, :]
                                        .broadcast_to((128, NH, NC // 2 * 2 * W)))
                ins.then_inc(s["st_init"], 1)

            def A_(n):
                if n == 1:
                    for part in range(3):
                        constant_rows(n, part)
                if n % 2 == 0:
                    dve.wait_ge(s["xnT_ok"], n + 1 + n // 2 + 1)
                    if n >= 2:
                        dve.wait_ge(s["vg_ps"], n // 2)
                    v.tensor_copy(xg[:, :, :], xnT[:, 0, None, XM:XM + PRE].broadcast_to((128, 8, PRE)))\
                        .then_inc(s["xg_ok"], 1)
                dve.wait_ge(s["kf_ok"], n + 1)
                if n % 2 == 0:
                    if n == 0:
                        dve.wait_ge(s["w_in"], 5 * 16)
                    v.tensor_tensor(kg[:, n // 2], kf[:, None, 0:PRE].broadcast_to((128, NH, PRE)),
                                    hsel_s[:, :, None].broadcast_to((128, NH, PRE)), ALU.mult)\
                        .then_inc(s["kg_ok"], 1)
                dve.wait_ge(s["kh_ok"], n + 1)
                link(v.tensor_tensor(kr, kf[:, :], kp[:, 0, :], ALU.subtract))
                v.tensor_copy(kp[:, 1, :], kr).then_inc(s["km_ok"], 1)
                dve.wait_ge(s["km_ok"], n + 1)
                v.tensor_tensor(kp[:, 2, :], kr, kp[:, 1, :], ALU.subtract).then_inc(s["kparts"], 1)
                if n % 2 == 0:
                    b = n // 2
                    dve.wait_ge(s["vg_ps"], b + 1)
                    dve.wait_ge(s["vones"], 4)
                    v.tensor_tensor(vg[:, b, :, :, 0:HD].rearrange("p g i d -> p (g i) d"),
                                    ring[:, 0, 0:D].rearrange("p (h d) -> p h d", d=HD),
                                    gsel_s[:, :, None].broadcast_to((128, NH, HD)), ALU.mult)\
                        .then_inc(s["vg_ok"], 1)
                    v.tensor_copy(vg[:, b, :, :, HD].rearrange("p g i -> p (g i)"), gsel_s[:, :])\
                        .then_inc(s["vg_ok"], 1)
                if n == 0:
                    constant_rows(n, 1)
                    constant_rows(n, 2)

            def unit_max(n, u):
                t, g = u // 5, u % 5
                i = NU * n + u
                dve.wait_ge(s["s1_ps"], i + 1)
                if g < 4:
                    v.tensor_reduce(m4[:, t, 4 * g:4 * g + 4], aux_bank(n, u)[:, :].rearrange("p (h k) -> p h k", h=4),
                                    AX.X, ALU.max).then_inc(s["max_ok"], 1)
                else:
                    v.tensor_reduce(mg[:, t, :], aux_bank(n, u)[:, 0:NH * PRE].rearrange("p (h k) -> p h k", h=NH),
                                    AX.X, ALU.max).then_inc(s["max_ok"], 1)

            def maxima(n):
                dve.wait_ge(s["max_ok"], NU * (n + 1))
                v.tensor_tensor(mt[:, :, :], m4[:, :, :], mg[:, :, :], ALU.max).then_inc(s["mt_ok"], 1)
                dve.wait_ge(s["mT_ps"], n + 1)
                if n >= 1:
                    dve.wait_ge(s["m_in"], 32 * n)
                    dve.wait_ge(s["pg_ps"], 2 * n)
                v.tensor_copy(mh[:, :], pa[0][0:NH, :]).then_inc(s["mhl"], 1)
                dve.wait_ge(s["mhl"], 2 * n + 1)
                v.tensor_tensor(ml[:, :], pa[0][0:NH, :], mh[:, :], ALU.subtract).then_inc(s["mhl"], 1)

            def C_(n):
                for u in range(NU):
                    unit_max(n, u)
                maxima(n)

            def D_(n):
                if n >= 1:
                    dve.wait_ge(s["mt_ok"], n)
                if n == NS - 1:
                    select(0, 0)
                    select(0, 1)
                for c in range(NC):
                    if n >= 1 and c == 1:
                        logits(n - 1)
                        if n == NS - 1:
                            place(0, 0)
                    if n + 1 < NS:
                        for u in units_at(n, c):
                            unit_max(n + 1, u)
                    if c % 4 == 3:
                        hf = c // 4
                        dve.wait_ge(s["pv_ok"], NC * n + 4 * (hf + 1))
                        if n >= 1:
                            dve.wait_ge(s["oT_ps"], NT * n)
                        v.tensor_copy(oS[:, hf, 2:4], pb[1][:, :].rearrange("p (g q) -> p g q", g=2))\
                            .then_inc(s["oS_ok"], 1)
                        if n == NS - 1 and hf == 0:
                            place(0, 1)
                if n + 1 < NS:
                    maxima(n + 1)

            def E_(n):
                for t in range(NT):
                    i = NT * n + t
                    dve.wait_ge(s["oT_ps"], i + 1)
                    o = pa[1 - t % 2][:, :].rearrange("p (h e) -> p h e", e=32)
                    if i >= 2:
                        dve.wait_ge(s["otok_ok"], i - 1)
                        dve.wait_ge(s["o2_ps"], i - 1)
                    link(v.reciprocal(rden[:, i % 2, :], o[:, :, HD]))
                    v.tensor_tensor(otok[:, i % 2], o[:, :, 0:HD], rden[:, i % 2, :, None].broadcast_to((128, NH, HD)),
                                    ALU.mult).then_inc(s["otok_ok"], 1)
                for name, value in normed:
                    dve.wait_ge(s[name], value)
                for t in range(NT):
                    i = NT * n + t
                    dve.wait_ge(s["att_ps"], i + 1)
                    v.tensor_tensor(x_s[:, n, t, :], ring[:, t, D:2 * D], x_s[:, n, t, :], ALU.add)\
                        .then_inc(s["x1_ok"], 1)
                    dve.wait_ge(s["x1_ok"], i + 1)
                    link(v.bn_stats(st6[:, t, :], x_s[:, n, t, :]))
                    last = v.bn_aggr(mv[:, t, :], st6[:, t, :])
                last.then_inc(s["stats2"], 1)
                if n < NS - 1:
                    second_norm(n)

            def second_norm(n):
                dve.wait_ge(s["rstd2_ok"], n + 1)
                dve.wait_ge(s["stats2"], n + 1)
                for t in range(NT):
                    v.tensor_scalar(xn2[:, n, t, :], x_s[:, n, t, :], mv[:, t, 0:1], rstd[:, t:t + 1],
                                    ALU.subtract, ALU.mult).then_inc(s["xn2_ok"], 1)
                normed[:] = [("xn2_ok", NT * (n + 1))]

            def logits(n):
                if n == 0:
                    dve.wait_ge(s["f_in"], 12 * 16)
                dve.wait_ge(s["lg_ps"], n + 1)
                v.tensor_tensor(lg[:, n // 2, (n % 2) * NT:(n % 2 + 1) * NT, :],
                                gate_bank(n)[:, 0:NT * E].rearrange("p (t e) -> p t e", t=NT),
                                gb_s[:, None, :].broadcast_to((128, NT, E)), ALU.add).then_inc(s["lg_ok"], 1)

            def bc(a):
                return a[:, :, None].broadcast_to((128, BT, E))

            def select(b, r):
                dve.wait_ge(s["lg_ok"], 2 * (b + 1))
                io = steps_s[:, None, 0:E].broadcast_to((128, BT, E))
                cur = lg2[:, :, :] if r else lg[:, b]
                link(v.tensor_reduce(top[:, r, :], cur, AX.X, ALU.max))
                link(v.tensor_tensor(tmp8[:, :, :], cur, bc(top[:, r, :]), ALU.is_lt))
                link(v.scalar_tensor_tensor(tmp8[:, :, :], tmp8[:, :, :], 16.0, io, ALU.mult, ALU.add))
                link(v.tensor_reduce(pk[:, :, r], tmp8[:, :, :], AX.X, ALU.min))
                link(v.tensor_tensor(oh[:, :, r, :], bc(pk[:, :, r]), io, ALU.is_equal))
                if r == 0:
                    link(v.scalar_tensor_tensor(lg2[:, :, :], oh[:, :, 0, :], -3.0e38, lg[:, b],
                                                ALU.mult, ALU.add))
                    return
                v.tensor_copy(ohb[:, :, :, :], oh[:, :, :, :]).then_inc(s["oh_ok"], 1)
                v.tensor_tensor(dif[:, :, 0:E], lg[:, b], bc(top[:, 0, :]), ALU.subtract)
                v.tensor_tensor(dif[:, :, E], top[:, 1, :], top[:, 0, :], ALU.subtract).then_inc(s["dif_ok"], 1)

            def place(b, part):
                if part == 1:
                    return blocks_and_values(b)
                before, total = count_bank(b)
                dve.wait_ge(s["pos_ps"], b + 1)
                link(v.tensor_copy(cnt[:, :], total))
                link(v.scalar_tensor_tensor(cmp_, steps_s[:, None, 0:BT].broadcast_to((128, 2 * E, BT)), 128.0,
                                            cnt[:, :, None].broadcast_to((128, 2 * E, BT)), ALU.mult, ALU.is_lt))
                link(v.tensor_reduce(nblk[:, :, :].rearrange("p r e -> p (r e)"), cmp_, AX.X, ALU.add))
                for r in range(2):
                    last = v.tensor_tensor(pre[:, r], nblk[:, r, None, :].broadcast_to((128, E, E)),
                                           upto_s[:, :, :], ALU.mult)
                link(last)
                link(v.tensor_reduce(endb[:, :, :], pre, AX.X, ALU.add))
                link(v.tensor_tensor(begb[:, :], endb[:, :, :].rearrange("p r e -> p (r e)"),
                                     nblk[:, :, :].rearrange("p r e -> p (r e)"), ALU.subtract))
                link(v.scalar_tensor_tensor(slot_of, begb[:, None, :].broadcast_to((128, BT, 2 * E)), 128.0,
                                            before.rearrange("p (t c) -> p t c", t=BT),
                                            ALU.mult, ALU.add))
                link(v.tensor_tensor(slot_of, slot_of, oh[:, :, :, :].rearrange("p t r e -> p t (r e)"), ALU.mult))
                link(v.tensor_reduce(posf[:, :, :], slot_of.rearrange("p t (r e) -> p t r e", r=2), AX.X, ALU.add))
                v.tensor_copy(pos[:, b], posf[:, :, :]).then_inc(s["pos_ok"], 1)

            def blocks_and_values(b):
                for r in range(2):
                    last = v.tensor_tensor(over[:, r], endb[:, r, None, :].broadcast_to((128, NBLK, E)),
                                           steps_s[:, 0:NBLK, None].broadcast_to((128, NBLK, E)), ALU.is_le)
                link(last)
                link(v.tensor_reduce(ebf[:, :, :], over, AX.X, ALU.add))
                v.tensor_scalar(eb[:, b, :, 0:NBLK], ebf[:, :, :], float(E - 1), 128.0, ALU.min, ALU.mult)\
                    .then_inc(s["eb_ok"], 1)
                dve.wait_ge(s["ex_ok"], b + 1)
                link(v.tensor_reduce(dn[:, :], ex[:, :, 0:E], AX.X, ALU.add))
                link(v.reciprocal(rdn[:, :], dn[:, :]))
                v.tensor_copy(val[:, b, :, 0], rdn[:, :])
                link(v.tensor_tensor(val[:, b, :, 1], ex[:, :, E], rdn[:, :], ALU.mult))

            def R_(_):
                beside = {0: [(second_norm, 3), (logits, 3), (select, 1, 0), (select, 1, 1),
                              (place, 1, 0), (place, 1, 1)]}
                for b in range(NB):
                    o = NBLK * (b + 1)
                    beside.update({o + 8: [(boost, b, 0)], o + 10: [(boost, b, 1)]})
                    for k in range(4):
                        beside[o + 11 + k] = [(weigh_first, b, k)]
                o = NBLK * 3
                for k in range(2):
                    beside[o + 6 + k] = [(weigh_second, 0, 0, k)]
                    beside[o + 8 + k] = [(second_stats, 0, 0, k)]
                    beside[o + 11 + k] = [(weigh_second, 0, 1, k)]
                    beside[o + 13 + k] = [(second_stats, 0, 1, k)]
                beside.update({o + 10: [(centre, 0)], o + 15: [(centre, 1)]})
                for st in range(ALL + 2):
                    if st == LENT:
                        dve.wait_ge(s["xT_ok"], LENT)
                    if st == LENT + 2:
                        dve.wait_ge(s["hT_ok"], LENT)
                    if st - 2 >= LENT:
                        hidden_copy(dve, v.tensor_copy, st - 2)
                    if LENT <= st < ALL:
                        token_copy(dve, v.tensor_copy, st)
                    for step, *args in beside.get(st, ()):
                        step(*args)

            def rows_in(q, hf):
                dve.wait_ge(s["yga_in" if hf == 0 else "ygb_in"], 16 * NT * (q + 1))

            def weigh(b, r, hf, pair):
                for t in range(2 * pair, 2 * pair + 2):
                    k = hf * NT + t
                    last = v.scalar_tensor_tensor(xn2[:, 2 * b + hf, t, :], yg[:, k, :], val[:, b, k, r:r + 1],
                                                  xn2[:, 2 * b + hf, t, :], ALU.mult, ALU.add)
                return last

            def boost(b, hf):
                rows_in(GATHERS.index(f"M{b}"), hf)
                if b == 1:
                    dve.wait_ge(s["xs_wr2"], 16 * BT)
                v.scalar_tensor_tensor(bst[:, hf * NT:(hf + 1) * NT, :], yg[:, hf * NT:(hf + 1) * NT, :], 0.5,
                                       xn2[:, 2 * b + hf], ALU.mult, ALU.add).then_inc(s["bst_ok"], 1)

            def weigh_first(b, k):
                dve.wait_ge(s["bst_ok"], 2 * b + k // 2 + 1)
                weigh(b, 0, k // 2, k % 2).then_inc(s["yg_used"], 1)

            def weigh_second(b, hf, k):
                q = GATHERS.index(f"N{b}")
                if k == 0:
                    rows_in(q, hf)
                    dve.wait_ge(s["yg_used"], 4 * q + 2 * hf)
                weigh(b, 1, hf, k).then_inc(s["yg_used"], 1)

            def second_stats(b, hf, k):
                n = 2 * b + hf
                dve.wait_ge(s["yg_used"], 4 * GATHERS.index(f"N{b}") + 2 * hf + 2)
                if b == 1:
                    dve.wait_ge(s["outs_ok"], hf + 1)
                for t in (2 * k, 2 * k + 1):
                    last = v.bn_stats(st6[:, t, :], xn2[:, n, t, :])
                link(last)
                for t in (2 * k, 2 * k + 1):
                    last = v.bn_aggr(mv3[:, hf, t, :], st6[:, t, :])
                last.then_inc(s["stats3"], 1)

            def centre(n):
                z = xn2[:, n]
                dve.wait_ge(s["stats3"], 2 * (n + 1))
                for t in range(NT):
                    last = v.scalar_tensor_tensor(z[:, t, :], z[:, t, :], mv3[:, n % 2, t, 0:1], gam_s[:, :],
                                                  ALU.subtract, ALU.mult)
                last.then_inc(s["z_ok"], 1)

            def result(n):
                z = xn2[:, n]
                dve.wait_ge(s["z_ok"], n + 1)
                dve.wait_ge(s["rstd3_ok"], n + 1)
                dve.wait_ge(s["xb_ok"], n + 1)
                for t in range(NT):
                    last = v.scalar_tensor_tensor(z[:, t, :], z[:, t, :], rstd3[:, n % 2, t:t + 1], x_s[:, n, t, :],
                                                  ALU.mult, ALU.add)
                last.then_inc(s["outs_ok"], 1)

            def N_(b):
                if b == 1:
                    for hf in range(2):
                        for k in range(2):
                            weigh_second(1, hf, k)
                        for k in range(2):
                            second_stats(1, hf, k)
                        centre(2 + hf)
                        result(2 + hf)

            run(L=L_, A=A_, C=C_, D=D_, E=E_, R=R_, N=N_)


_WEIGHTS = ["L0_attn_x", "L0_attn_w_qkv", "L0_attn_w_out", "L0_ffn_gate_W", "L0_ffn_gate_b", "L0_ffn_W1",
            "L0_ffn_b1", "L0_ffn_W2", "L0_ffn_b2", "L0_ffn_ln_gamma", "L0_ffn_ln_beta"]


def _constants(np, bf16):
    D, NH, HD, W, PRE, ST, E = 128, 16, 8, 64, 16, 512, 8
    BIG = -(2.0 ** 100)
    col = np.arange(ST) % W
    row = np.arange(W)[:, None]
    kconst = np.zeros((128, 2, 8, 2, W), np.float32)
    kconst[W:, :, :, 0] = np.where(row.T <= row, BIG, 0.0)[:, None, None, :]
    kconst[W:, :, :, 1] = np.where(row.T > row, BIG, 0.0)[:, None, None, :]
    kconst[48, 0, 0, 0] = BIG
    kconst[48, 0, 0, 1, :PRE] = BIG
    kconst[48, 0, 1, 0, :PRE] = BIG
    kconst = kconst.reshape(128, 2, 2 * ST)
    kconst[49:51] = -1.0
    qconst = np.zeros((128, ST), np.float32)
    qconst[48] = 1.0
    qconst[W:] = (col[None, :] == row)
    maxsel = np.zeros((NH, 2, 128), np.float32)
    for h in range(NH):
        maxsel[h, h // 8, (h % 8) * PRE:(h % 8 + 1) * PRE] = -1.0
    q, k = np.arange(128)[:, None], np.arange(PRE)[None, :]
    after = np.where(k > q, BIG, 0.0).astype(np.float32)
    prefmask = np.tile(after, (1, NH))
    prefmaskT = np.tile(np.where(q < PRE, after, 0.0), (1, 8))
    p = np.arange(128)
    headsel = (p[:, None] // HD == np.arange(NH)[None, :]).astype(np.float32)
    selgrp = (p[:, None] // PRE == np.arange(NH)[None, :] % 8).astype(np.float32)
    upper = (p[:, None] < p[None, :]).astype(np.float32)
    upto = np.broadcast_to(np.arange(E)[None, :] <= np.arange(E)[:, None], (128, E, E)).astype(np.float32)
    steps = np.broadcast_to(np.arange(16), (128, 16)).astype(np.float32)
    ident = np.eye(128, dtype=np.float32)
    return {"ident": ident, "identb": ident.astype(bf16), "kconst": kconst.astype(bf16),
            "qconst": qconst.astype(bf16), "maxsel": maxsel.astype(bf16), "prefmask": prefmask.astype(bf16),
            "prefmaskT": prefmaskT.astype(bf16), "headsel": headsel, "selgrp": selgrp,
            "upper": upper.astype(bf16), "onesb": np.ones((128, 128), bf16), "upto": upto, "steps": steps}


def kernel(**inputs):
    import numpy as np
    import ml_dtypes
    import concourse.bacc as bacc
    from concourse import mybir
    from concourse.bass_utils import run_bass_kernel_spmd

    a = {n: np.asarray(inputs[n]) for n in _WEIGHTS}
    x, wqkv, wo, gw, gb, w1, b1, w2, b2, gamma, beta = (a[n] for n in _WEIGHTS)
    arrays = {
        "x": x.reshape(2048, 128), "wqkvT": np.ascontiguousarray(wqkv.T), "woT": np.ascontiguousarray(wo.T),
        "gateW": gw, "gateb": gb, "W1": w1, "W2": w2,
        "bias": np.concatenate([b1[:, 0:128], b1[:, 128:256], b2]).reshape(128, 24),
        "gamma": gamma, "beta": beta,
    }
    arrays.update(_constants(np, ml_dtypes.bfloat16))
    nc = bacc.Bacc("TRN2", target_bir_lowering=False, num_devices=1)
    args = [nc.dram_tensor("in_" + n, v.shape, mybir.dt.from_np(v.dtype), kind="ExternalInput").ap()
            for n, v in arrays.items()]
    out = nc.dram_tensor("out_0", (2048, 128), mybir.dt.float32, kind="ExternalOutput").ap()
    preln_block_kernel(nc, *args, out)
    r = run_bass_kernel_spmd(nc, [{"in_" + n: np.ascontiguousarray(v) for n, v in arrays.items()}], core_ids=[0])
    return r.results[0]["out_0"].reshape(2, 1024, 128)
```
